# Optimizing a Trainium2 kernel written in Bass

```python
import numpy as np
import jax
import jax.numpy as jnp

def _softmax(x, axis=-1):
    return jax.nn.softmax(x, axis=axis)

def _gelu(x):
    return jax.nn.gelu(x, approximate=True)

def _silu(x):
    return jax.nn.silu(x)

def _sigmoid(x):
    return jax.nn.sigmoid(x)

def _layernorm(x, axis=-1, eps=1e-05):
    m = jnp.mean(x, axis=axis, keepdims=True)
    v = jnp.var(x, axis=axis, keepdims=True)
    return (x - m) / jnp.sqrt(v + eps)

def _scatter_add(tgt, idx, src, axis=0):
    return tgt.at[idx].add(src)

def _segment_sum(src, seg, n):
    return jax.ops.segment_sum(src, seg, n)
kernel_name = 'mk_dlrm_tower_d1_rec_r8_b3a1e7'

def setup_inputs(seed: int=0):
    np.random.seed(seed)
    _w = jnp.asarray

    def _rec_inputs():
        import jax
        import jax.numpy as jnp
        _tk = jax.random.key(seed)
        dense_ctx = jax.random.normal(jax.random.fold_in(_tk, 190), (512, 16), jnp.float32)
        ids = jnp.stack([jax.random.randint(jax.random.fold_in(_tk, 200 + f), (512,), 0, v, jnp.int32) for f, v in enumerate([12500, 1250, 1250, 1000, 12500, 1000, 1250, 1250, 1000, 12500, 1000, 12500, 125000, 1000, 12500, 125000, 12500, 1000, 1000, 125000, 125000, 12500, 1000, 125000, 125000, 12500])], axis=1)
        tbl_0 = 0.05 * jax.random.normal(jax.random.fold_in(_tk, 500 + 0), (12500, 32), jnp.float32)
        tbl_1 = 0.05 * jax.random.normal(jax.random.fold_in(_tk, 500 + 1), (1250, 32), jnp.float32)
        tbl_2 = 0.05 * jax.random.normal(jax.random.fold_in(_tk, 500 + 2), (1250, 32), jnp.float32)
        tbl_3 = 0.05 * jax.random.normal(jax.random.fold_in(_tk, 500 + 3), (1000, 32), jnp.float32)
        tbl_4 = 0.05 * jax.random.normal(jax.random.fold_in(_tk, 500 + 4), (12500, 32), jnp.float32)
        tbl_5 = 0.05 * jax.random.normal(jax.random.fold_in(_tk, 500 + 5), (1000, 32), jnp.float32)
        tbl_6 = 0.05 * jax.random.normal(jax.random.fold_in(_tk, 500 + 6), (1250, 32), jnp.float32)
        tbl_7 = 0.05 * jax.random.normal(jax.random.fold_in(_tk, 500 + 7), (1250, 32), jnp.float32)
        tbl_8 = 0.05 * jax.random.normal(jax.random.fold_in(_tk, 500 + 8), (1000, 32), jnp.float32)
        tbl_9 = 0.05 * jax.random.normal(jax.random.fold_in(_tk, 500 + 9), (12500, 32), jnp.float32)
        tbl_10 = 0.05 * jax.random.normal(jax.random.fold_in(_tk, 500 + 10), (1000, 32), jnp.float32)
        tbl_11 = 0.05 * jax.random.normal(jax.random.fold_in(_tk, 500 + 11), (12500, 32), jnp.float32)
        tbl_12 = 0.05 * jax.random.normal(jax.random.fold_in(_tk, 500 + 12), (125000, 32), jnp.float32)
        tbl_13 = 0.05 * jax.random.normal(jax.random.fold_in(_tk, 500 + 13), (1000, 32), jnp.float32)
        tbl_14 = 0.05 * jax.random.normal(jax.random.fold_in(_tk, 500 + 14), (12500, 32), jnp.float32)
        tbl_15 = 0.05 * jax.random.normal(jax.random.fold_in(_tk, 500 + 15), (125000, 32), jnp.float32)
        tbl_16 = 0.05 * jax.random.normal(jax.random.fold_in(_tk, 500 + 16), (12500, 32), jnp.float32)
        tbl_17 = 0.05 * jax.random.normal(jax.random.fold_in(_tk, 500 + 17), (1000, 32), jnp.float32)
        tbl_18 = 0.05 * jax.random.normal(jax.random.fold_in(_tk, 500 + 18), (1000, 32), jnp.float32)
        tbl_19 = 0.05 * jax.random.normal(jax.random.fold_in(_tk, 500 + 19), (125000, 32), jnp.float32)
        tbl_20 = 0.05 * jax.random.normal(jax.random.fold_in(_tk, 500 + 20), (125000, 32), jnp.float32)
        tbl_21 = 0.05 * jax.random.normal(jax.random.fold_in(_tk, 500 + 21), (12500, 32), jnp.float32)
        tbl_22 = 0.05 * jax.random.normal(jax.random.fold_in(_tk, 500 + 22), (1000, 32), jnp.float32)
        tbl_23 = 0.05 * jax.random.normal(jax.random.fold_in(_tk, 500 + 23), (125000, 32), jnp.float32)
        tbl_24 = 0.05 * jax.random.normal(jax.random.fold_in(_tk, 500 + 24), (125000, 32), jnp.float32)
        tbl_25 = 0.05 * jax.random.normal(jax.random.fold_in(_tk, 500 + 25), (12500, 32), jnp.float32)
        _rk = jax.random.fold_in(_tk, 7)
        W_top1 = 0.0606339 * jax.random.normal(jax.random.fold_in(_tk, 801), (272, 512), jnp.float32)
        W_top2 = 0.0441942 * jax.random.normal(jax.random.fold_in(_tk, 802), (512, 256), jnp.float32)
        W_top3 = 0.0625 * jax.random.normal(jax.random.fold_in(_tk, 803), (256, 1), jnp.float32)
        b_top1 = jnp.zeros((512,), jnp.float32)
        b_top2 = jnp.zeros((256,), jnp.float32)
        return (dense_ctx, ids, tbl_0, tbl_1, tbl_2, tbl_3, tbl_4, tbl_5, tbl_6, tbl_7, tbl_8, tbl_9, tbl_10, tbl_11, tbl_12, tbl_13, tbl_14, tbl_15, tbl_16, tbl_17, tbl_18, tbl_19, tbl_20, tbl_21, tbl_22, tbl_23, tbl_24, tbl_25, W_top1, b_top1, W_top2, b_top2, W_top3)
    dense_ctx, ids, tbl_0, tbl_1, tbl_2, tbl_3, tbl_4, tbl_5, tbl_6, tbl_7, tbl_8, tbl_9, tbl_10, tbl_11, tbl_12, tbl_13, tbl_14, tbl_15, tbl_16, tbl_17, tbl_18, tbl_19, tbl_20, tbl_21, tbl_22, tbl_23, tbl_24, tbl_25, W_top1, b_top1, W_top2, b_top2, W_top3 = _rec_inputs()

    def _L0_rec_setup():
        import jax, jax.numpy as jnp
        import numpy as np
        M_FIELDS = 26
        H1 = 128
        H2 = 128
        BATCH = 256
        EMB_K = 32

        def _cin_layer(x_prev, x0, W, b):
            return jnp.einsum('bik,bjk,hij->bhk', x_prev, x0, W) + b[None, :, None]
        key = jax.random.key(seed)
        k0, k1, k2, k3, k4 = jax.random.split(key, 5)
        inputs = jax.random.normal(k0, (BATCH, M_FIELDS, EMB_K), dtype=jnp.float32)
        W1 = jax.random.normal(k1, (H1, M_FIELDS, M_FIELDS), dtype=jnp.float32) * 0.05
        b1 = jax.random.normal(k2, (H1,), dtype=jnp.float32) * 0.05
        W2 = jax.random.normal(k3, (H2, H1, M_FIELDS), dtype=jnp.float32) * 0.05
        b2 = jax.random.normal(k4, (H2,), dtype=jnp.float32) * 0.05
        return {'inputs': inputs, 'W1': W1, 'b1': b1, 'W2': W2, 'b2': b2}
    _L0_rec_all = _L0_rec_setup()
    _L0_rec_in = {k: v for k, v in _L0_rec_all.items() if k in ('W1', 'b1', 'W2', 'b2')}
    del _L0_rec_all
    return {'dense_ctx': dense_ctx, 'ids': ids, 'tbl_0': tbl_0, 'tbl_1': tbl_1, 'tbl_2': tbl_2, 'tbl_3': tbl_3, 'tbl_4': tbl_4, 'tbl_5': tbl_5, 'tbl_6': tbl_6, 'tbl_7': tbl_7, 'tbl_8': tbl_8, 'tbl_9': tbl_9, 'tbl_10': tbl_10, 'tbl_11': tbl_11, 'tbl_12': tbl_12, 'tbl_13': tbl_13, 'tbl_14': tbl_14, 'tbl_15': tbl_15, 'tbl_16': tbl_16, 'tbl_17': tbl_17, 'tbl_18': tbl_18, 'tbl_19': tbl_19, 'tbl_20': tbl_20, 'tbl_21': tbl_21, 'tbl_22': tbl_22, 'tbl_23': tbl_23, 'tbl_24': tbl_24, 'tbl_25': tbl_25, 'W_top1': W_top1, 'b_top1': b_top1, 'W_top2': W_top2, 'b_top2': b_top2, 'W_top3': W_top3, 'L0_rec_W1': _L0_rec_in['W1'], 'L0_rec_b1': _L0_rec_in['b1'], 'L0_rec_W2': _L0_rec_in['W2'], 'L0_rec_b2': _L0_rec_in['b2']}

def reference(dense_ctx, ids, tbl_0, tbl_1, tbl_2, tbl_3, tbl_4, tbl_5, tbl_6, tbl_7, tbl_8, tbl_9, tbl_10, tbl_11, tbl_12, tbl_13, tbl_14, tbl_15, tbl_16, tbl_17, tbl_18, tbl_19, tbl_20, tbl_21, tbl_22, tbl_23, tbl_24, tbl_25, W_top1, b_top1, W_top2, b_top2, W_top3, L0_rec_W1, L0_rec_b1, L0_rec_W2, L0_rec_b2):
    import jax
    import jax.numpy as jnp

    def _L0_rec_ref(inputs, W1, b1, W2, b2):
        import jax, jax.numpy as jnp
        import numpy as np
        M_FIELDS = 26
        H1 = 128
        H2 = 128
        BATCH = 256
        EMB_K = 32

        def _cin_layer(x_prev, x0, W, b):
            return jnp.einsum('bik,bjk,hij->bhk', x_prev, x0, W) + b[None, :, None]
        x1 = _cin_layer(inputs, inputs, W1, b1)
        x2 = _cin_layer(x1, inputs, W2, b2)
        res = jnp.concatenate([x1, x2], axis=1)
        return jnp.sum(res, axis=-1)
    e = jnp.stack([tbl_0[ids[:, 0]], tbl_1[ids[:, 1]], tbl_2[ids[:, 2]], tbl_3[ids[:, 3]], tbl_4[ids[:, 4]], tbl_5[ids[:, 5]], tbl_6[ids[:, 6]], tbl_7[ids[:, 7]], tbl_8[ids[:, 8]], tbl_9[ids[:, 9]], tbl_10[ids[:, 10]], tbl_11[ids[:, 11]], tbl_12[ids[:, 12]], tbl_13[ids[:, 13]], tbl_14[ids[:, 14]], tbl_15[ids[:, 15]], tbl_16[ids[:, 16]], tbl_17[ids[:, 17]], tbl_18[ids[:, 18]], tbl_19[ids[:, 19]], tbl_20[ids[:, 20]], tbl_21[ids[:, 21]], tbl_22[ids[:, 22]], tbl_23[ids[:, 23]], tbl_24[ids[:, 24]], tbl_25[ids[:, 25]]], axis=1)
    z = _L0_rec_ref(e, L0_rec_W1, L0_rec_b1, L0_rec_W2, L0_rec_b2)
    z = z.reshape(z.shape[0], -1)
    h = jnp.concatenate([z, dense_ctx], axis=1)
    h = jnp.maximum(h @ W_top1 + b_top1, 0.0)
    h = jnp.maximum(h @ W_top2 + b_top2, 0.0)
    y = h @ W_top3
    return y

_drawn_inputs = setup_inputs


def setup_inputs(seed=0):
    import zlib

    import numpy as np

    out = dict(_drawn_inputs(seed))
    spreads = {'b_top1': (0.0, 2.0), 'b_top2': (0.0, 0.8)}
    factors = {'tbl_0': 8.0,
     'tbl_1': 8.0,
     'tbl_2': 8.0,
     'tbl_3': 8.0,
     'tbl_4': 8.0,
     'tbl_5': 8.0,
     'tbl_6': 8.0,
     'tbl_7': 8.0,
     'tbl_8': 8.0,
     'tbl_9': 8.0,
     'tbl_10': 8.0,
     'tbl_11': 8.0,
     'tbl_12': 8.0,
     'tbl_13': 8.0,
     'tbl_14': 8.0,
     'tbl_15': 8.0,
     'tbl_16': 8.0,
     'tbl_17': 8.0,
     'tbl_18': 8.0,
     'tbl_19': 8.0,
     'tbl_20': 8.0,
     'tbl_21': 7.507,
     'tbl_22': 8.0,
     'tbl_23': 8.0,
     'tbl_24': 8.0,
     'tbl_25': 8.0,
     'L0_rec_W1': 8.0,
     'L0_rec_W2': 4.035,
     'dense_ctx': 6.093}
    for name, (base, spread) in spreads.items():
        noise = np.random.default_rng([zlib.crc32(name.encode()), seed]).standard_normal(out[name].shape)
        drawn = base * np.exp(spread * noise) if base else spread * noise
        out[name] = jnp.asarray(drawn.astype(out[name].dtype))
    for name, factor in factors.items():
        out[name] = (out[name] * factor).astype(out[name].dtype)
    return out
```

```python
from contextlib import ExitStack

import concourse.bass as bass
from concourse import mybir
from concourse.alu_op_type import AluOpType as ALU


F32 = mybir.dt.float32
I32 = mybir.dt.int32
ACT = mybir.ActivationFunctionType

P = 128
NF = 26
NH = NF // 2
K = 32
B = 512
G = B // P
NT = P // 4
NPR = NH * (NH + 1) // 2
ONE_A = NPR
SGL = (NPR + 1, NPR)
MCOL = (NPR + 1 + NH, NPR + NH)
KV = (NPR + 1, NPR)
BLK = 4
NB = NT // BLK
RING = 4
GR = NH * NF + NH * NH
GC = 4
GP = -(-GR // GC)
GLAST = GR - (GC - 1) * GP
H = 128
CTX = 16
D1, D2 = 512, 256
M1, M2 = D1 // P, D2 // P


def pair_off(p):
    return NH + p * (NH - 1) - p * (p - 1) // 2


def build(nc, a, y):
    with ExitStack() as ctx:
        def sb(name, shape, dt=F32):
            return ctx.enter_context(nc.sbuf_tensor(name, shape, dt))

        def sem(name):
            return ctx.enter_context(nc.semaphore(name))

        idx = sb("idx", [P, G, NF], I32)
        emb = sb("emb", [P, G, NF * K])
        ework = sb("ework", [P, NF * K])
        L = [sb("l_a", [P, NT, MCOL[0]]), sb("l_b", [P, NT, MCOL[1]])]
        R = sb("r", [P, NT, 4, NF])
        T = [sb("t_a", [P, NF, P]), sb("t_b", [P, NF, P])]
        gram = sb("gram", [P, GC, P])
        ident = sb("ident", [P, P])
        w1 = sb("w1", [P, NF, NF])
        w2 = sb("w2", [P, H, NF])
        w2t = sb("w2t", [P, NF, H])
        w1p = [sb("w1p_a", [P, KV[0]]), sb("w1p_b", [P, KV[1]])]
        w1ab = sb("w1ab", [P, NH, NH])
        w1g = sb("w1g", [P, GR])
        mab = sb("mab", [P, NF, NH, NH])
        cross = [sb("cross_a", [P, NH, NPR]), sb("cross_b", [P, NH, NPR])]
        V = [sb("v_a", [P, NF, H]), sb("v_b", [P, NF, H])]
        wg = sb("wg", [P, GC, H])
        rows = sb("rows", [10, P])
        cols = sb("cols", [P, 10])
        kb = sb("kb", [P, 2])
        ctx_in = sb("ctx_in", [P, G, CTX])
        ctx_t = sb("ctx_t", [CTX, G, P])
        wt1 = sb("wt1", [P, 2, D1])
        wt1c = sb("wt1c", [CTX, D1])
        wt2 = sb("wt2", [P, M1, D2])
        z = sb("z", [P, 2, P])
        h1 = sb("h1", [P, M1, P])
        h2 = sb("h2", [P, M2, P])
        yrow = sb("yrow", [1, B])
        gram_dram = nc.dram_tensor("gram_scratch", [GR, P], F32, kind="Internal").ap()

        ring = [ctx.enter_context(nc.psum_tensor(f"ring{i}", [P, 512], F32)) for i in range(RING)]
        zp = [ctx.enter_context(nc.psum_tensor(f"z{i + 1}p", [P, 512], F32))[:, 0:P] for i in range(2)]
        h1p = ctx.enter_context(nc.psum_tensor("h1p", [P, M1, P], F32))
        h2y = ctx.enter_context(nc.psum_tensor("h2y", [P, 4, P], F32))
        h2p, yp = h2y[:, 0:M2, :], h2y[0:1, M2, :]

        ids_in = sem("ids_in")
        w2_in = sem("w2_in")
        w1_in = sem("w1_in")
        rows_in = sem("rows_in")
        ctx_loaded = sem("ctx_loaded")
        wt_in = sem("wt_in")
        gathered = [[sem(f"gathered{g}{'ab'[c]}") for c in range(2)] for g in range(G)]
        half_in = sem("half_in")
        ident_step = sem("ident_step")
        pre_done = sem("pre_done")
        pre_out = sem("pre_out")
        w1_ready = sem("w1_ready")
        cross_ready = sem("cross_ready")
        ones_set = sem("ones_set")
        r_zero = sem("r_zero")
        e_moved = sem("e_moved")
        singles = sem("singles")
        r_ready = sem("r_ready")
        pairs = sem("pairs")
        t_done = sem("t_done")
        t_out = sem("t_out")
        gram_out = sem("gram_out")
        gram_in = sem("gram_in")
        z2_done = sem("z2_done")
        z1_done = sem("z1_done")
        z_ready = sem("z_ready")
        h1_done = sem("h1_done")
        h1_ready = sem("h1_ready")
        h2_done = sem("h2_done")
        h2_ready = sem("h2_ready")
        y_done = sem("y_done")
        y_ready = sem("y_ready")
        y_out = sem("y_out")
        kb_ready = sem("kb_ready")

        def jblocks():
            return [(j, min(4, NF - j)) for j in range(0, NF, 4)]

        def xblocks():
            return [(x, min(3, NF - x)) for x in range(0, NF, 3)]

        pre = [("small", 0, 0)] + [("w2t", j, n) for j, n in jblocks()] + [("ctx", 0, 0)]
        pre += [("mab", x, n) for x, n in xblocks()]
        pre += [("wg", 0, 0)]
        pre += [("v", c, jb) for c in range(2) for jb in jblocks()]
        at = {b: n for n, b in enumerate(pre)}
        W2T_OUT = at[("w2t",) + jblocks()[-1]] + 1
        MAB_OUT = {0: at[("mab",) + xblocks()[(NH - 1) // 3]] + 1, 1: at[("mab",) + xblocks()[-1]] + 1}

        block = ctx.enter_context(nc.Block())

        @block.sync
        def _(sp):
            sp.dma_start(idx[:, :, :], a["ids"].rearrange("(g p) f -> p g f", p=P)).then_inc(ids_in, 16)
            sp.dma_start(w2[:, :, :], a["L0_rec_W2"]).then_inc(w2_in, 16)
            sp.dma_start(w1[:, :, :], a["L0_rec_W1"]).then_inc(w1_in, 16)
            sp.dma_start(wt1[:, :, :], a["W_top1"][0:2 * P, :].rearrange("(c p) n -> p c n", p=P)).then_inc(wt_in, 16)
            sp.dma_start(wt1c[:, :], a["W_top1"][2 * P:2 * P + CTX, :]).then_inc(wt_in, 16)
            sp.dma_start(wt2[:, :, :], a["W_top2"].rearrange("(c p) n -> p c n", p=P)).then_inc(wt_in, 16)
            for g in range(G):
                for c in range(2):
                    sp.wait_ge(gathered[g][c], 16 * NH)
                    sp.sem_inc(half_in, 1)
            sp.wait_ge(y_ready, G)
            sp.dma_start(y.rearrange("b o -> o b"), yrow[:, :]).then_inc(y_out, 16)
            sp.wait_ge(y_out, 16)

        @block.gpsimd
        def _(pool):
            pool.memset(ident[:, :], 0.0).then_inc(ident_step, 1)
            pool.wait_ge(ident_step, 1)
            pool.affine_select(out=ident[:, :], in_=ident[:, :], compare_op=ALU.not_equal, fill=1.0, base=0,
                               pattern=[[-1, P]], channel_multiplier=1).then_inc(ident_step, 1)
            pool.wait_ge(ids_in, 16)
            for g in range(G):
                for f in range(NF):
                    pool.indirect_dma_start(
                        out=emb[:, g, f * K:(f + 1) * K], out_offset=None, in_=a[f"tbl_{f}"][:, :],
                        in_offset=bass.IndirectOffsetOnAxis(ap=idx[:, g, f:f + 1], axis=0),
                    ).then_inc(gathered[g][f // NH], 16)

        @block.vector
        def _(dve):
            dve.wait_ge(w1_in, 16)
            dve.tensor_tensor(w1ab[:, :, :], w1[:, 0:NH, NH:NF],
                              w1[:, NH:NF, 0:NH].rearrange("p v u -> p u v"), ALU.add).then_inc(w1_ready, 1)
            w1flat = w1[:, :, :].rearrange("p u v -> p (u v)")
            for c in range(2):
                o = c * NH
                d0 = o * (NF + 1)
                dve.tensor_copy(w1p[c][:, 0:NH], w1flat[:, d0:d0 + (NH - 1) * (NF + 1) + 1:NF + 1])
                for p in range(NH - 1):
                    n = NH - 1 - p
                    dve.tensor_tensor(w1p[c][:, pair_off(p):pair_off(p) + n], w1[:, o + p, o + p + 1:o + NH],
                                      w1[:, o + p + 1:o + NH, o + p], ALU.add)
            dve.wait_ge(pre_out, 1)
            dve.tensor_copy(w1p[0][:, NPR:NPR + 1], cols[:, 8:9]).then_inc(w1_ready, 1)
            dve.wait_ge(w1_ready, 1)
            wga = w1g[:, 0:NH * NF].rearrange("p (u v) -> p u v", v=NF)
            dve.tensor_copy(wga[:, :, 0:NH], w1[:, 0:NH, 0:NH])
            dve.tensor_copy(wga[:, :, NH:NF], w1ab[:, :, :])
            dve.tensor_copy(w1g[:, NH * NF:GR].rearrange("p (u v) -> p u v", v=NH),
                            w1[:, NH:NF, NH:NF]).then_inc(w1_ready, 1)
            dve.memset(L[0][:, :, ONE_A:ONE_A + 1], 1.0).then_inc(ones_set, 1)
            dve.memset(R[:, :, :, :], 0.0).then_inc(r_zero, 1)

            def cross_terms(c):
                dve.wait_ge(pre_out, MAB_OUT[c])
                out = cross[c]
                diag = out[:, :, 0:NH]
                if c == 0:
                    src = mab[:, 0:NH, :, :].rearrange("p x u v -> p (x u) v")[:, 0:(NH - 1) * (NH + 1) + 1:NH + 1, :]
                    dve.tensor_copy(diag.rearrange("p j x -> p x j"), src).then_inc(cross_ready, 1)
                else:
                    for j in range(NH):
                        srcj = flat_diag(j)
                        last = dve.tensor_copy(out[:, j, 0:NH], srcj)
                    last.then_inc(cross_ready, 1)
                for p in range(NH - 1):
                    n = NH - 1 - p
                    dst = out[:, :, pair_off(p):pair_off(p) + n].rearrange("p j q -> p q j")
                    if c == 0:
                        one = mab[:, p, p + 1:NH, :]
                        two = mab[:, p + 1:NH, p, :]
                    else:
                        one = mab[:, NH + p, :, p + 1:NH].rearrange("p j q -> p q j")
                        two = mab[:, NH + p + 1:NF, :, p]
                    last = dve.tensor_tensor(dst, one, two, ALU.add)
                last.then_inc(cross_ready, 1)

            def flat_diag(j):
                full = mab[:, :, :, :].rearrange("p x u v -> p (x u v)")
                s = NH * NH + 1
                first = NH * NH * NH + j * NH
                return full[:, first:first + (NH - 1) * s + 1:s]

            def build_half(g, c, first):
                e = slice(c * NH * K, (c + 1) * NH * K)
                dve.wait_ge(half_in, 2 * g + c + 1)
                if not first:
                    dve.wait_ge(singles, 2 * g + c - 1)
                dve.tensor_copy(ework[:, e], emb[:, g, e] if isinstance(g, int) else emb[:, bass.ds(g, 1), e].rearrange("p a n -> p (a n)")).then_inc(e_moved, 1)
                if not first:
                    dve.wait_ge(t_done, 2 * NB * (g - 1) + NB * (c + 1))
                dve.wait_ge(e_moved, 2 * g + c + 1)
                sg = L[c][:, :, SGL[c]:SGL[c] + NH]
                dve.transpose(sg.rearrange("p t f -> p f t"), ework[:, e]).then_inc(singles, 1)
                if first:
                    dve.wait_ge(r_zero, 1)
                elif c == 0:
                    dve.wait_ge(t_done, 2 * NB * g)
                dve.wait_ge(singles, 2 * g + c + 1)
                for q in range(4):
                    s = slice(K * q, K * (q + 1))
                    last = dve.tensor_copy(R[s, :, q, c * NH:(c + 1) * NH], L[c][s, :, SGL[c]:SGL[c] + NH])
                last.then_inc(r_ready, 1)
                dve.tensor_tensor(L[c][:, :, 0:NH], sg, sg, ALU.mult)
                for p in range(NH - 1):
                    n = NH - 1 - p
                    last = dve.tensor_tensor(
                        L[c][:, :, pair_off(p):pair_off(p) + n], sg[:, :, p + 1:NH],
                        sg[:, :, p:p + 1].to_broadcast([P, NT, n]), ALU.mult)
                last.then_inc(pairs, 1)

            cross_terms(0)
            cross_terms(1)
            build_half(0, 0, True)
            build_half(0, 1, True)
            with dve.Fori(1, G) as g:
                build_half(g, 0, False)
                build_half(g, 1, False)

        @block.tensor
        def _(pe):
            def free_bank(n):
                if n >= RING:
                    pe.wait_ge(pre_out, n - RING + 1)

            pe.wait_ge(ident_step, 2)
            for n, (kind, c, m) in enumerate(pre):
                free_bank(n)
                ps = ring[n % RING]
                if kind == "small":
                    pe.wait_ge(rows_in, 16 * 5)
                    last = pe.transpose(ps[:, 0:10], rows[:, :], ident[0:10, 0:10])
                elif kind == "w2t":
                    if c == 0:
                        pe.wait_ge(w2_in, 16)
                    for i in range(m):
                        last = pe.transpose(ps[:, i * H:(i + 1) * H], w2[:, :, c + i], ident[:, :])
                elif kind == "ctx":
                    pe.wait_ge(ctx_loaded, 16)
                    for g in range(G):
                        last = pe.transpose(ps[0:CTX, g * P:(g + 1) * P], ctx_in[:, g, :], ident[:, :])
                elif kind == "mab":
                    if c == 0:
                        pe.wait_ge(w1_ready, 1)
                        pe.wait_ge(pre_out, W2T_OUT)
                    for i in range(m):
                        last = pe.matmul(ps[:, i * NH * NH:(i + 1) * NH * NH], w2t[:, c + i, :],
                                         w1ab[:, :, :].rearrange("p u v -> p (u v)"), start=True, stop=True)
                elif kind == "wg":
                    pe.wait_ge(w1_ready, 3)
                    for i in range(GC):
                        w = GP if i < GC - 1 else GLAST
                        last = pe.transpose(ps[0:w, i * H:(i + 1) * H], w1g[:, i * GP:i * GP + w], ident[:, :])
                else:
                    j0, nj = m
                    if j0 == 0:
                        pe.wait_ge(cross_ready, 2 * (c + 1))
                    other = [j for j in range(j0, j0 + nj) if (j >= NH) == (c == 0)]
                    last = pe.matmul(ps[0:KV[c], 0:nj * H], w1p[c][:, :],
                                     w2t[:, j0:j0 + nj, :].rearrange("p j h -> p (j h)"),
                                     start=True, stop=True)
                    for j in other:
                        last = pe.matmul(ps[0:NPR, (j - j0) * H:(j - j0 + 1) * H],
                                         cross[c][:, j - (NH if c == 0 else 0), :], ident[:, :],
                                         start=False, stop=True, skip_group_check=True)
                last.then_inc(pre_done, 1)

            def t_block(g, n, first):
                c, blk = divmod(n, NB)
                if blk == 0:
                    pe.wait_ge(pairs, 2 * g + c + 1)
                    if c == 0:
                        pe.wait_ge(r_ready, 2 * g + 2)
                if not (first and n < RING):
                    pe.wait_ge(t_out, 2 * NB * g + n - RING + 1)
                ps = ring[n % RING]
                for i in range(BLK):
                    t = blk * BLK + i
                    last = pe.matmul(ps[0:MCOL[c], i * 4 * NF:(i + 1) * 4 * NF], L[c][:, t, :],
                                     R[:, t, :, :].rearrange("p q f -> p (q f)"), start=True, stop=True)
                last.then_inc(t_done, 1)

            def z_group(g, first):
                if not first:
                    pe.wait_ge(z_ready, 2 * g)
                for c in range(2):
                    pe.wait_ge(t_out, 2 * NB * g + NB * (c + 1))
                    for j in range(NF):
                        last = pe.matmul(zp[1], V[c][0:KV[c], j, :], T[c][0:KV[c], j, :],
                                         start=(c == 0 and j == 0), stop=(c == 1 and j == NF - 1))
                last.then_inc(z2_done, 1)
                pe.wait_ge(gram_in, 32 * (g + 1))
                for i in range(GC):
                    w = GP if i < GC - 1 else GLAST
                    last = pe.matmul(zp[0], wg[0:w, i, :], gram[0:w, i, :], start=(i == 0), stop=(i == GC - 1))
                last.then_inc(z1_done, 1)

            def layer1(g):
                pe.wait_ge(z_ready, 2 * (g + 1))
                for m in range(M1):
                    s = slice(m * P, (m + 1) * P)
                    cg = ctx_t[:, g, :] if isinstance(g, int) else ctx_t[:, bass.ds(g, 1), :].rearrange("p a n -> p (a n)")
                    pe.matmul(h1p[:, m, :], wt1c[:, s], cg, start=True, stop=False)
                    pe.matmul(h1p[:, m, :], wt1[:, 0, s], z[:, 0, :], start=False, stop=False)
                    last = pe.matmul(h1p[:, m, :], wt1[:, 1, s], z[:, 1, :], start=False, stop=True)
                last.then_inc(h1_done, 1)

            def layer2(g):
                pe.wait_ge(h1_ready, M1 * (g + 1))
                for m in range(M2):
                    for kc in range(M1):
                        last = pe.matmul(h2p[:, m, :], wt2[:, kc, m * P:(m + 1) * P], h1[:, kc, :],
                                         start=(kc == 0), stop=(kc == M1 - 1))
                last.then_inc(h2_done, 1)

            def layer3(g):
                pe.wait_ge(h2_ready, M2 * (g + 1))
                for kc in range(M2):
                    last = pe.matmul(yp, cols[:, 6 + kc:7 + kc], h2[:, kc, :], start=(kc == 0), stop=(kc == M2 - 1))
                last.then_inc(y_done, 1)

            pe.wait_ge(wt_in, 48)
            pe.wait_ge(pre_out, len(pre))
            for n in range(2 * NB):
                t_block(0, n, True)
            z_group(0, True)
            with pe.Fori(1, G) as g:
                for n in range(2 * NB):
                    t_block(g, n, False)
                    if n == 2:
                        layer1(g - 1)
                    if n == 7:
                        layer2(g - 1)
                    if n == 11:
                        layer3(g - 1)
                z_group(g, False)
            layer1(G - 1)
            layer2(G - 1)
            layer3(G - 1)

        @block.scalar
        def _(act):
            act.dma_start(rows[0:4, :], a["b_top1"].rearrange("(r n) -> r n", n=P)).then_inc(rows_in, 16)
            act.dma_start(rows[4:6, :], a["b_top2"].rearrange("(r n) -> r n", n=P)).then_inc(rows_in, 16)
            act.dma_start(rows[6:8, :], a["W_top3"].rearrange("(r n) o -> r (n o)", n=P)).then_inc(rows_in, 16)
            act.dma_start(rows[8:9, :], a["L0_rec_b1"].rearrange("(r n) -> r n", n=P)).then_inc(rows_in, 16)
            act.dma_start(rows[9:10, :], a["L0_rec_b2"].rearrange("(r n) -> r n", n=P)).then_inc(rows_in, 16)
            act.dma_start(ctx_in[:, :, :], a["dense_ctx"].rearrange("(g p) c -> p g c", p=P)).then_inc(ctx_loaded, 16)
            for n, (kind, c, m) in enumerate(pre):
                ps = ring[n % RING]
                act.wait_ge(pre_done, n + 1)
                if kind == "small":
                    last = act.copy(cols[:, :], ps[:, 0:10])
                elif kind == "w2t":
                    last = act.copy(w2t[:, c:c + m, :].rearrange("p j h -> p (j h)"), ps[:, 0:m * H])
                elif kind == "ctx":
                    for g in range(G):
                        last = act.copy(ctx_t[:, g, :].rearrange("p (t q) -> p t q", q=4),
                                        ps[0:CTX, g * P:(g + 1) * P].rearrange("p (q t) -> p t q", q=4))
                elif kind == "mab":
                    last = act.copy(mab[:, c:c + m, :, :].rearrange("p x u v -> p (x u v)"), ps[:, 0:m * NH * NH])
                elif kind == "wg":
                    act.copy(wg[0:GP, 0:GC - 1, :].rearrange("p c h -> p (c h)"), ps[0:GP, 0:(GC - 1) * H])
                    last = act.copy(wg[0:GLAST, GC - 1, :], ps[0:GLAST, (GC - 1) * H:GC * H])
                else:
                    j0, nj = m
                    last = act.copy(V[c][0:KV[c], j0:j0 + nj, :].rearrange("p j h -> p (j h)"), ps[0:KV[c], 0:nj * H])
                last.then_inc(pre_out, 1)
            act.mul(kb[:, :], cols[:, 8:10], float(K)).then_inc(kb_ready, 1)
            act.wait_ge(kb_ready, 1)

            def copy_block(g, n):
                c, blk = divmod(n, NB)
                act.wait_ge(t_done, 2 * NB * g + n + 1)
                src = ring[n % RING][0:MCOL[c], 0:BLK * 4 * NF].rearrange("p (x j) -> p j x", j=NF)
                act.copy(T[c][0:MCOL[c], :, blk * 4 * BLK:(blk + 1) * 4 * BLK], src).then_inc(t_out, 1)

            def gram_turn(g, first):
                act.wait_ge(t_out, 2 * NB * (g + 1))
                act.dma_start(gram_dram[0:NH * NF, :].rearrange("(u v) b -> u v b", v=NF),
                              T[0][SGL[0]:SGL[0] + NH, :, :]).then_inc(gram_out, 16)
                act.dma_start(gram_dram[NH * NF:GR, :].rearrange("(u v) b -> u v b", v=NH),
                              T[1][SGL[1]:SGL[1] + NH, NH:NF, :]).then_inc(gram_out, 16)
                if not first:
                    act.wait_ge(z1_done, g)
                act.wait_ge(gram_out, 32 * (g + 1))
                act.dma_start(gram[0:GP, 0:GC - 1, :], gram_dram[0:(GC - 1) * GP, :].rearrange("(c p) b -> p c b", p=GP)).then_inc(gram_in, 16)
                act.dma_start(gram[0:GLAST, GC - 1, :], gram_dram[(GC - 1) * GP:GR, :]).then_inc(gram_in, 16)

            def z_copy(g, first):
                act.wait_ge(z2_done, g + 1)
                if not first:
                    act.wait_ge(h1_done, g)
                act.activation(z[:, 1, :], zp[1], ACT.Identity, bias=kb[:, 1:2]).then_inc(z_ready, 1)
                act.wait_ge(z1_done, g + 1)
                act.activation(z[:, 0, :], zp[0], ACT.Identity, bias=kb[:, 0:1]).then_inc(z_ready, 1)

            def relu1(g, first):
                act.wait_ge(h1_done, g + 1)
                if not first:
                    act.wait_ge(h2_done, g)
                for m in range(M1):
                    act.activation(h1[:, m, :], h1p[:, m, :], ACT.Relu, bias=cols[:, m:m + 1]).then_inc(h1_ready, 1)

            def relu2(g, first):
                act.wait_ge(h2_done, g + 1)
                if not first:
                    act.wait_ge(y_done, g)
                for m in range(M2):
                    act.activation(h2[:, m, :], h2p[:, m, :], ACT.Relu, bias=cols[:, 4 + m:5 + m]).then_inc(h2_ready, 1)

            def y_copy(g):
                act.wait_ge(y_done, g + 1)
                yg = yrow[:, g * P:(g + 1) * P] if isinstance(g, int) else yrow[:, bass.ds(g * P, P)]
                act.copy(yg.rearrange("o (q t) -> o t q", q=4), yp.rearrange("o (t q) -> o t q", q=4)).then_inc(y_ready, 1)

            for n in range(2 * NB):
                copy_block(0, n)
            gram_turn(0, True)
            z_copy(0, True)

            def group(g, first_mlp):
                for n in range(2 * NB):
                    copy_block(g, n)
                    if n == 2:
                        relu1(g - 1, first_mlp)
                    if n == 7:
                        relu2(g - 1, first_mlp)
                    if n == 11:
                        y_copy(g - 1)
                gram_turn(g, False)
                z_copy(g, False)

            group(1, True)
            with act.Fori(2, G) as g:
                group(g, False)
            relu1(G - 1, False)
            relu2(G - 1, False)
            y_copy(G - 1)


_INS = (["dense_ctx", "ids"] + [f"tbl_{f}" for f in range(NF)]
        + ["W_top1", "b_top1", "W_top2", "b_top2", "W_top3", "L0_rec_W1", "L0_rec_b1", "L0_rec_W2", "L0_rec_b2"])


def kernel(**inputs):
    import numpy as _np
    import concourse.bacc as _bacc
    from concourse import mybir as _mybir
    from concourse.bass_utils import run_bass_kernel_spmd as _run

    nc = _bacc.Bacc("TRN2", target_bir_lowering=False, num_devices=1)
    arrays, args = {}, {}
    for name in _INS:
        x = _np.ascontiguousarray(inputs[name])
        arrays[f"in_{name}"] = x
        args[name] = nc.dram_tensor(f"in_{name}", x.shape, _mybir.dt.from_np(x.dtype), kind="ExternalInput").ap()
    y = nc.dram_tensor("out_y", (B, 1), _mybir.dt.float32, kind="ExternalOutput").ap()
    build(nc, args, y)
    r = _run(nc, [arrays], core_ids=[0])
    return r.results[0]["out_y"]
```

```python
from contextlib import ExitStack

import concourse.bass as bass
from concourse import mybir
from concourse.alu_op_type import AluOpType as ALU


F32 = mybir.dt.float32
I32 = mybir.dt.int32
ACT = mybir.ActivationFunctionType

P = 128
NF = 26
NH = NF // 2
K = 32
B = 512
G = B // P
NT = P // 4
Q1 = (NH + 1) // 2
Q2 = NH - Q1
NIN = NH + Q1 * (Q1 - 1) // 2 + Q2 * (Q2 - 1) // 2
SGL = NIN
ONE = SGL + NH
HALF = 64
ACR = HALF
NX = Q1 * Q2
MC = ACR + NX
assert ONE + 2 == HALF
BLK = 4
NB = NT // BLK
RING = 4
MIX = NX + NH * NH
GR = NH * NF + NH * NH
GC = 4
GP = -(-GR // GC)
GLAST = GR - (GC - 1) * GP
H = 128
CTX = 16
D1, D2 = 512, 256
M1, M2 = D1 // P, D2 // P


def inner_pairs():
    at, out = NH, []
    for q_first, q_end in ((0, Q1), (Q1, NH)):
        for p in range(q_first, q_end - 1):
            n = q_end - 1 - p
            out.append((at, p, p + 1, n))
            at += n
    assert at == NIN
    return out


def build(nc, a, y):
    with ExitStack() as ctx:
        def sb(name, shape, dt=F32):
            return ctx.enter_context(nc.sbuf_tensor(name, shape, dt))

        def sem(name):
            return ctx.enter_context(nc.semaphore(name))

        idx = sb("idx", [P, G, NF], I32)
        emb = sb("emb", [P, G, NF * K])
        ework = sb("ework", [P, NF * K])
        L = [sb(f"l_{x}", [P, NT, MC]) for x in "ab"]
        R = sb("r", [P, NT, 4, NF])
        t_a = sb("t_a", [P, NF, P])
        t_b = sb("t_b", [P, NH, P])
        gram = sb("gram", [P, GC, P])
        ident = sb("ident", [P, P])
        w1 = sb("w1", [P, NF, NF])
        w2 = sb("w2", [P, H, NF])
        w2t = sb("w2t", [P, NF, H])
        w1p = [sb(f"w1p_{x}", [P, MC]) for x in "ab"]
        w1m = sb("w1m", [P, MIX + NX])
        w1x = [w1m[:, 0:NX], w1m[:, MIX:MIX + NX]]
        w1ab = w1m[:, NX:MIX].rearrange("p (u v) -> p u v", v=NH)
        w1g = sb("w1g", [P, GR])
        mix = sb("mix", [P, NF, MIX])
        cross = [sb(f"cross_{x}", [P, NH, MC]) for x in "ab"]
        cross_own = sb("cross_own", [P, NH, P])
        v_a = sb("v_a", [P, NF, H])
        v_b = sb("v_b", [P, NH, H])
        wg = sb("wg", [P, GC, H])
        rows = sb("rows", [10, P])
        cols = sb("cols", [P, 10])
        kb = sb("kb", [P, 2])
        ctx_in = sb("ctx_in", [P, G, CTX])
        ctx_t = sb("ctx_t", [CTX, G, P])
        wt1 = sb("wt1", [P, 2, D1])
        wt1c = sb("wt1c", [CTX, D1])
        wt2 = sb("wt2", [P, M1, D2])
        z = sb("z", [P, 2, P])
        h1 = sb("h1", [P, M1, P])
        h2 = sb("h2", [P, M2, P])
        yrow = sb("yrow", [1, B])
        gram_dram = nc.dram_tensor("gram_scratch", [GR, P], F32, kind="Internal").ap()

        ring = [ctx.enter_context(nc.psum_tensor(f"ring{i}", [P, 512], F32)) for i in range(RING)]
        zp = [ctx.enter_context(nc.psum_tensor(f"z{i + 1}p", [P, 512], F32))[:, 0:P] for i in range(2)]
        h1p = ctx.enter_context(nc.psum_tensor("h1p", [P, M1, P], F32))
        h2y = ctx.enter_context(nc.psum_tensor("h2y", [P, 4, P], F32))
        h2p, yp = h2y[:, 0:M2, :], h2y[0:1, M2, :]

        ids_in = sem("ids_in")
        w2_in = sem("w2_in")
        w1_in = sem("w1_in")
        rows_in = sem("rows_in")
        ctx_loaded = sem("ctx_loaded")
        wt_in = sem("wt_in")
        gathered = [[sem(f"gathered{g}{'ab'[c]}") for c in range(2)] for g in range(G)]
        half_in = sem("half_in")
        ident_step = sem("ident_step")
        pre_done = sem("pre_done")
        pre_out = sem("pre_out")
        w1_ready = sem("w1_ready")
        cross_ready = sem("cross_ready")
        zeroed = sem("zeroed")
        e_moved = sem("e_moved")
        singles = sem("singles")
        r_ready = sem("r_ready")
        pairs = sem("pairs")
        t_done = sem("t_done")
        t_out = sem("t_out")
        gram_out = sem("gram_out")
        gram_in = sem("gram_in")
        z2_done = sem("z2_done")
        z1_done = sem("z1_done")
        z_ready = sem("z_ready")
        h1_done = sem("h1_done")
        h1_ready = sem("h1_ready")
        h2_done = sem("h2_done")
        h2_ready = sem("h2_ready")
        y_done = sem("y_done")
        y_ready = sem("y_ready")
        y_out = sem("y_out")
        kb_ready = sem("kb_ready")

        def cut(count, most):
            return [(j, min(most, count - j)) for j in range(0, count, most)]

        xpairs = [(x0 + x, n) for x0 in (0, NH) for x, n in cut(NH, 2)]
        pre = [("w2t", j, n) for j, n in cut(NF, 4)] + [("small", 0, 0)]
        pre += [("mix", x, n) for x, n in xpairs]
        pre += [("ctx", 0, 0), ("wg", 0, 0)]
        pre += [(kind, j, n) for kind in ("va", "vb", "own") for j, n in cut(NH, 4)]
        at = {b: n for n, b in enumerate(pre)}
        W2T_OUT = at[("w2t",) + cut(NF, 4)[-1]] + 1
        MIX_OUT = [at[("mix",) + xpairs[len(xpairs) // 2 - 1]] + 1, at[("mix",) + xpairs[-1]] + 1]

        block = ctx.enter_context(nc.Block())

        @block.sync
        def _(sp):
            sp.dma_start(idx[:, :, :], a["ids"].rearrange("(g p) f -> p g f", p=P)).then_inc(ids_in, 16)
            sp.dma_start(w2[:, :, :], a["L0_rec_W2"]).then_inc(w2_in, 16)
            sp.dma_start(w1[:, :, :], a["L0_rec_W1"]).then_inc(w1_in, 16)
            sp.dma_start(wt1[:, :, :], a["W_top1"][0:2 * P, :].rearrange("(c p) n -> p c n", p=P)).then_inc(wt_in, 16)
            sp.dma_start(wt1c[:, :], a["W_top1"][2 * P:2 * P + CTX, :]).then_inc(wt_in, 16)
            sp.dma_start(wt2[:, :, :], a["W_top2"].rearrange("(c p) n -> p c n", p=P)).then_inc(wt_in, 16)
            for g in range(G):
                for c in range(2):
                    sp.wait_ge(gathered[g][c], 16 * NH)
                    sp.sem_inc(half_in, 1)
            sp.wait_ge(y_ready, G)
            sp.dma_start(y.rearrange("b o -> o b"), yrow[:, :]).then_inc(y_out, 16)
            sp.wait_ge(y_out, 16)

        @block.gpsimd
        def _(pool):
            pool.memset(ident[:, :], 0.0).then_inc(ident_step, 1)
            pool.wait_ge(ident_step, 1)
            pool.affine_select(out=ident[:, :], in_=ident[:, :], compare_op=ALU.not_equal, fill=1.0, base=0,
                               pattern=[[-1, P]], channel_multiplier=1).then_inc(ident_step, 1)
            pool.wait_ge(ids_in, 16)
            for g in range(G):
                for f in range(NF):
                    pool.indirect_dma_start(
                        out=emb[:, g, f * K:(f + 1) * K], out_offset=None, in_=a[f"tbl_{f}"][:, :],
                        in_offset=bass.IndirectOffsetOnAxis(ap=idx[:, g, f:f + 1], axis=0),
                    ).then_inc(gathered[g][f // NH], 16)

        @block.vector
        def _(dve):
            dve.wait_ge(w1_in, 16)
            dve.tensor_tensor(w1ab, w1[:, 0:NH, NH:NF], w1[:, NH:NF, 0:NH].rearrange("p v u -> p u v"), ALU.add)
            for c in range(2):
                o = c * NH
                last = dve.tensor_tensor(w1x[c].rearrange("p (u v) -> p u v", v=Q2), w1[:, o:o + Q1, o + Q1:o + NH],
                                         w1[:, o + Q1:o + NH, o:o + Q1].rearrange("p v u -> p u v"), ALU.add)
            last.then_inc(w1_ready, 1)
            dve.wait_ge(w1_ready, 1)
            w1flat = w1[:, :, :].rearrange("p u v -> p (u v)")
            for c in range(2):
                o = c * NH
                d0 = o * (NF + 1)
                dve.tensor_copy(w1p[c][:, 0:NH], w1flat[:, d0:d0 + (NH - 1) * (NF + 1) + 1:NF + 1])
                for col, p, q, n in inner_pairs():
                    dve.tensor_tensor(w1p[c][:, col:col + n], w1[:, o + p, o + q:o + q + n],
                                      w1[:, o + q:o + q + n, o + p], ALU.add)
                dve.memset(w1p[c][:, SGL:ONE if c == 0 else ACR], 0.0)
                dve.tensor_copy(w1p[c][:, ACR:MC], w1x[c])
            dve.memset(w1p[0][:, ONE + 1:ACR], 0.0)
            wga = w1g[:, 0:NH * NF].rearrange("p (u v) -> p u v", v=NF)
            dve.tensor_copy(wga[:, :, 0:NH], w1[:, 0:NH, 0:NH])
            dve.tensor_copy(wga[:, :, NH:NF], w1ab)
            dve.tensor_copy(w1g[:, NH * NF:GR].rearrange("p (u v) -> p u v", v=NH), w1[:, NH:NF, NH:NF])
            for c in range(2):
                dve.memset(L[c][:, :, ONE:ONE + 1], 1.0)
                dve.memset(L[c][:, :, ONE + 1:ACR], 0.0)
                dve.memset(cross[c][:, :, SGL:ACR], 0.0)
            dve.memset(cross_own[:, :, :], 0.0)
            dve.memset(R[:, :, :, :], 0.0).then_inc(zeroed, 1)
            dve.wait_ge(pre_out, at[("small", 0, 0)] + 1)
            dve.tensor_copy(w1p[0][:, ONE:ONE + 1], cols[:, 8:9]).then_inc(w1_ready, 1)

            def mixed(c, x0, x1, quarters):
                first, n = (0, NH * NH) if not quarters else (NH * NH, NX)
                if c == 0:
                    first = NX - first if not quarters else 0
                v = mix[:, c * NH + x0:c * NH + x1, first:first + n]
                return v.rearrange("p x (u v) -> p x u v", v=NH if not quarters else Q2)

            def cross_terms(c):
                dve.wait_ge(pre_out, MIX_OUT[c])
                if c == 0:
                    dve.wait_ge(zeroed, 1)

                def m(x, xn, u, un):
                    v = mixed(c, x, x + xn, False)
                    return v[:, :, u:u + un, :] if c == 0 else v[:, :, :, u:u + un].rearrange("p x j u -> p x u j")

                def sums(dst, x, xn, u, un):
                    return dve.tensor_tensor(dst, m(x, xn, u, un), m(u, un, x, xn).rearrange("p q x j -> p x q j"), ALU.add)

                out = cross[c]
                for p in range(NH):
                    dve.tensor_copy(out[:, :, p], m(p, 1, p, 1).rearrange("p a b j -> p (a b j)"))
                for col, p, q, n in inner_pairs():
                    sums(out[:, :, col:col + n].rearrange("p j (x q) -> p x q j", x=1), p, 1, q, n)
                for p in range(Q1):
                    col = ACR + p * Q2
                    last = sums(out[:, :, col:col + Q2].rearrange("p j (x q) -> p x q j", x=1), p, 1, Q1, Q2)
                last.then_inc(cross_ready, 1)

            def own_terms(c):
                r = c * HALF
                for quarter, (x0, x1) in enumerate(((0, Q1), (Q1, NH))):
                    js = slice(Q1, NH) if quarter == 0 else slice(0, Q1)

                    def m(x, xn, u, un):
                        v = mixed(c, x, x + xn, True)
                        u -= x0
                        return v[:, :, u:u + un, :] if quarter == 0 else v[:, :, :, u:u + un].rearrange("p x j u -> p x u j")

                    for p in range(x0, x1):
                        dve.tensor_copy(cross_own[:, js, r + p], m(p, 1, p, 1).rearrange("p a b j -> p (a b j)"))
                    for col, p, q, n in inner_pairs():
                        if x0 <= p < x1:
                            last = dve.tensor_tensor(
                                cross_own[:, js, r + col:r + col + n].rearrange("p j (x q) -> p x q j", x=1),
                                m(p, 1, q, n), m(q, n, p, 1).rearrange("p q x j -> p x q j"), ALU.add)
                last.then_inc(cross_ready, 1)

            def build_half(g, c, first):
                e = slice(c * NH * K, (c + 1) * NH * K)
                dve.wait_ge(half_in, 2 * g + c + 1)
                if not first:
                    dve.wait_ge(singles, 2 * g + c - 1)
                dve.tensor_copy(ework[:, e], emb[:, g, e] if isinstance(g, int) else emb[:, bass.ds(g, 1), e].rearrange("p a n -> p (a n)")).then_inc(e_moved, 1)
                if not first:
                    dve.wait_ge(t_done, 2 * NB * (g - 1) + NB * (c + 1))
                dve.wait_ge(e_moved, 2 * g + c + 1)
                sg = L[c][:, :, SGL:SGL + NH]
                dve.transpose(sg.rearrange("p t f -> p f t"), ework[:, e]).then_inc(singles, 1)
                if not first and c == 0:
                    dve.wait_ge(t_done, 2 * NB * g)
                dve.wait_ge(singles, 2 * g + c + 1)
                for q in range(4):
                    s = slice(K * q, K * (q + 1))
                    last = dve.tensor_copy(R[s, :, q, c * NH:(c + 1) * NH], L[c][s, :, SGL:SGL + NH])
                last.then_inc(r_ready, 1)
                dve.tensor_tensor(L[c][:, :, 0:NH], sg, sg, ALU.mult)
                for col, p, q, n in inner_pairs() + [(ACR + p * Q2, p, Q1, Q2) for p in range(Q1)]:
                    last = dve.tensor_tensor(L[c][:, :, col:col + n], sg[:, :, q:q + n],
                                             sg[:, :, p:p + 1].to_broadcast([P, NT, n]), ALU.mult)
                last.then_inc(pairs, 1)

            cross_terms(0)
            cross_terms(1)
            own_terms(0)
            own_terms(1)
            build_half(0, 0, True)
            build_half(0, 1, True)
            with dve.Fori(1, G) as g:
                build_half(g, 0, False)
                build_half(g, 1, False)

        @block.tensor
        def _(pe):
            def free_bank(n):
                if n >= RING:
                    pe.wait_ge(pre_out, n - RING + 1)

            pe.wait_ge(ident_step, 2)
            for n, (kind, c, m) in enumerate(pre):
                free_bank(n)
                ps = ring[n % RING]
                if kind == "small":
                    pe.wait_ge(rows_in, 16 * 5)
                    last = pe.transpose(ps[:, 0:10], rows[:, :], ident[0:10, 0:10])
                elif kind == "w2t":
                    if c == 0:
                        pe.wait_ge(w2_in, 16)
                    for i in range(m):
                        last = pe.transpose(ps[:, i * H:(i + 1) * H], w2[:, :, c + i], ident[:, :])
                elif kind == "ctx":
                    pe.wait_ge(ctx_loaded, 16)
                    for g in range(G):
                        last = pe.transpose(ps[0:CTX, g * P:(g + 1) * P], ctx_in[:, g, :], ident[:, :])
                elif kind == "mix":
                    if c == 0:
                        pe.wait_ge(w1_ready, 1)
                        pe.wait_ge(pre_out, W2T_OUT)
                    o = 0 if c < NH else NX
                    for i in range(m):
                        last = pe.matmul(ps[:, i * MIX:(i + 1) * MIX], w2t[:, c + i, :], w1m[:, o:o + MIX],
                                         start=True, stop=True)
                elif kind == "wg":
                    pe.wait_ge(w1_ready, 2)
                    for i in range(GC):
                        w = GP if i < GC - 1 else GLAST
                        last = pe.transpose(ps[0:w, i * H:(i + 1) * H], w1g[:, i * GP:i * GP + w], ident[:, :])
                else:
                    if c == 0:
                        pe.wait_ge(cross_ready, {"va": 1, "vb": 2, "own": 4}[kind])

                    def w2_of(half):
                        return w2t[:, half * NH + c:half * NH + c + m, :].rearrange("p j h -> p (j h)")

                    if kind == "own":
                        for half in range(2):
                            pe.matmul(ps[half * HALF:(half + 1) * HALF, 0:m * H], w1p[half][:, 0:HALF], w2_of(half),
                                      start=True, stop=True)
                        terms = cross_own
                    else:
                        half = 0 if kind == "va" else 1
                        pe.matmul(ps[0:MC, 0:m * H], w1p[half][:, :], w2_of(1 - half), start=True, stop=True)
                        terms = cross[half]
                    for i in range(m):
                        w = terms[:, c + i, :]
                        last = pe.matmul(ps[0:w.shape[1], i * H:(i + 1) * H], w, ident[:, :],
                                         start=False, stop=True, skip_group_check=True)
                last.then_inc(pre_done, 1)

            def t_block(g, n, first):
                c, blk = divmod(n, NB)
                if blk == 0:
                    pe.wait_ge(pairs, 2 * g + c + 1)
                    if c == 0:
                        pe.wait_ge(r_ready, 2 * g + 2)
                if not (first and n < RING):
                    pe.wait_ge(t_out, 2 * NB * g + n - RING + 1)
                ps = ring[n % RING]
                for i in range(BLK):
                    t = blk * BLK + i
                    last = pe.matmul(ps[0:MC, i * 4 * NF:(i + 1) * 4 * NF], L[c][:, t, :],
                                     R[:, t, :, :].rearrange("p q f -> p (q f)"), start=True, stop=True)
                last.then_inc(t_done, 1)

            def z_group(g, first):
                if not first:
                    pe.wait_ge(z_ready, 2 * g)
                pe.wait_ge(t_out, 2 * NB * g + NB)
                for j in range(NH, NF):
                    pe.matmul(zp[1], v_a[0:MC, j, :], t_a[0:MC, j, :], start=(j == NH), stop=False)
                pe.wait_ge(t_out, 2 * NB * (g + 1))
                for j in range(NH):
                    pe.matmul(zp[1], v_b[0:MC, j, :], t_b[0:MC, j, :], start=False, stop=False)
                for j in range(NH):
                    last = pe.matmul(zp[1], v_a[:, j, :], t_a[:, j, :], start=False, stop=(j == NH - 1))
                last.then_inc(z2_done, 1)
                pe.wait_ge(gram_in, 32 * (g + 1))
                for i in range(GC):
                    w = GP if i < GC - 1 else GLAST
                    last = pe.matmul(zp[0], wg[0:w, i, :], gram[0:w, i, :], start=(i == 0), stop=(i == GC - 1))
                last.then_inc(z1_done, 1)

            def layer1(g):
                pe.wait_ge(z_ready, 2 * (g + 1))
                for m in range(M1):
                    s = slice(m * P, (m + 1) * P)
                    cg = ctx_t[:, g, :] if isinstance(g, int) else ctx_t[:, bass.ds(g, 1), :].rearrange("p a n -> p (a n)")
                    pe.matmul(h1p[:, m, :], wt1c[:, s], cg, start=True, stop=False)
                    pe.matmul(h1p[:, m, :], wt1[:, 0, s], z[:, 0, :], start=False, stop=False)
                    last = pe.matmul(h1p[:, m, :], wt1[:, 1, s], z[:, 1, :], start=False, stop=True)
                last.then_inc(h1_done, 1)

            def layer2(g):
                pe.wait_ge(h1_ready, M1 * (g + 1))
                for m in range(M2):
                    for kc in range(M1):
                        last = pe.matmul(h2p[:, m, :], wt2[:, kc, m * P:(m + 1) * P], h1[:, kc, :],
                                         start=(kc == 0), stop=(kc == M1 - 1))
                last.then_inc(h2_done, 1)

            def layer3(g):
                pe.wait_ge(h2_ready, M2 * (g + 1))
                for kc in range(M2):
                    last = pe.matmul(yp, cols[:, 6 + kc:7 + kc], h2[:, kc, :], start=(kc == 0), stop=(kc == M2 - 1))
                last.then_inc(y_done, 1)

            pe.wait_ge(wt_in, 48)
            pe.wait_ge(pre_out, len(pre))
            for n in range(2 * NB):
                t_block(0, n, True)
            z_group(0, True)
            with pe.Fori(1, G) as g:
                for n in range(2 * NB):
                    t_block(g, n, False)
                    if n == 2:
                        layer1(g - 1)
                    if n == 7:
                        layer2(g - 1)
                    if n == 11:
                        layer3(g - 1)
                z_group(g, False)
            layer1(G - 1)
            layer2(G - 1)
            layer3(G - 1)

        @block.scalar
        def _(act):
            act.dma_start(rows[0:4, :], a["b_top1"].rearrange("(r n) -> r n", n=P)).then_inc(rows_in, 16)
            act.dma_start(rows[4:6, :], a["b_top2"].rearrange("(r n) -> r n", n=P)).then_inc(rows_in, 16)
            act.dma_start(rows[6:8, :], a["W_top3"].rearrange("(r n) o -> r (n o)", n=P)).then_inc(rows_in, 16)
            act.dma_start(rows[8:9, :], a["L0_rec_b1"].rearrange("(r n) -> r n", n=P)).then_inc(rows_in, 16)
            act.dma_start(rows[9:10, :], a["L0_rec_b2"].rearrange("(r n) -> r n", n=P)).then_inc(rows_in, 16)
            act.dma_start(ctx_in[:, :, :], a["dense_ctx"].rearrange("(g p) c -> p g c", p=P)).then_inc(ctx_loaded, 16)
            for n, (kind, c, m) in enumerate(pre):
                ps = ring[n % RING]
                act.wait_ge(pre_done, n + 1)
                if kind == "small":
                    last = act.copy(cols[:, :], ps[:, 0:10])
                elif kind == "w2t":
                    last = act.copy(w2t[:, c:c + m, :].rearrange("p j h -> p (j h)"), ps[:, 0:m * H])
                elif kind == "ctx":
                    for g in range(G):
                        last = act.copy(ctx_t[:, g, :].rearrange("p (t q) -> p t q", q=4),
                                        ps[0:CTX, g * P:(g + 1) * P].rearrange("p (q t) -> p t q", q=4))
                elif kind == "mix":
                    last = act.copy(mix[:, c:c + m, :].rearrange("p x w -> p (x w)"), ps[:, 0:m * MIX])
                elif kind == "wg":
                    act.copy(wg[0:GP, 0:GC - 1, :].rearrange("p c h -> p (c h)"), ps[0:GP, 0:(GC - 1) * H])
                    last = act.copy(wg[0:GLAST, GC - 1, :], ps[0:GLAST, (GC - 1) * H:GC * H])
                else:
                    r = P if kind == "own" else MC
                    dst = {"va": v_a[0:r, NH + c:NH + c + m, :], "vb": v_b[0:r, c:c + m, :], "own": v_a[:, c:c + m, :]}[kind]
                    last = act.copy(dst.rearrange("p j h -> p (j h)"), ps[0:r, 0:m * H])
                last.then_inc(pre_out, 1)
            act.mul(kb[:, :], cols[:, 8:10], float(K)).then_inc(kb_ready, 1)
            act.wait_ge(kb_ready, 1)

            def copy_block(g, n):
                c, blk = divmod(n, NB)
                act.wait_ge(t_done, 2 * NB * g + n + 1)
                src = ring[n % RING][:, 0:BLK * 4 * NF].rearrange("p (x j) -> p j x", j=NF)
                s = slice(blk * 4 * BLK, (blk + 1) * 4 * BLK)
                if c == 0:
                    act.copy(t_a[0:MC, :, s], src[0:MC, :, :]).then_inc(t_out, 1)
                else:
                    act.copy(t_b[0:MC, :, s], src[0:MC, 0:NH, :])
                    act.wait_ge(t_out, 2 * NB * g + blk + 1)
                    act.copy(t_a[HALF:P, 0:NH, s], src[0:HALF, NH:NF, :]).then_inc(t_out, 1)

            def gram_turn(g, first):
                act.wait_ge(t_out, 2 * NB * (g + 1))
                act.dma_start(gram_dram[0:NH * NF, :].rearrange("(u v) b -> u v b", v=NF),
                              t_a[SGL:SGL + NH, :, :]).then_inc(gram_out, 16)
                act.dma_start(gram_dram[NH * NF:GR, :].rearrange("(u v) b -> u v b", v=NH),
                              t_a[HALF + SGL:HALF + SGL + NH, 0:NH, :]).then_inc(gram_out, 16)
                if not first:
                    act.wait_ge(z1_done, g)
                act.wait_ge(gram_out, 32 * (g + 1))
                act.dma_start(gram[0:GP, 0:GC - 1, :], gram_dram[0:(GC - 1) * GP, :].rearrange("(c p) b -> p c b", p=GP)).then_inc(gram_in, 16)
                act.dma_start(gram[0:GLAST, GC - 1, :], gram_dram[(GC - 1) * GP:GR, :]).then_inc(gram_in, 16)

            def z_copy(g, first):
                act.wait_ge(z2_done, g + 1)
                if not first:
                    act.wait_ge(h1_done, g)
                act.activation(z[:, 1, :], zp[1], ACT.Identity, bias=kb[:, 1:2]).then_inc(z_ready, 1)
                act.wait_ge(z1_done, g + 1)
                act.activation(z[:, 0, :], zp[0], ACT.Identity, bias=kb[:, 0:1]).then_inc(z_ready, 1)

            def relu1(g, first):
                act.wait_ge(h1_done, g + 1)
                if not first:
                    act.wait_ge(h2_done, g)
                for m in range(M1):
                    act.activation(h1[:, m, :], h1p[:, m, :], ACT.Relu, bias=cols[:, m:m + 1]).then_inc(h1_ready, 1)

            def relu2(g, first):
                act.wait_ge(h2_done, g + 1)
                if not first:
                    act.wait_ge(y_done, g)
                for m in range(M2):
                    act.activation(h2[:, m, :], h2p[:, m, :], ACT.Relu, bias=cols[:, 4 + m:5 + m]).then_inc(h2_ready, 1)

            def y_copy(g):
                act.wait_ge(y_done, g + 1)
                yg = yrow[:, g * P:(g + 1) * P] if isinstance(g, int) else yrow[:, bass.ds(g * P, P)]
                act.copy(yg.rearrange("o (q t) -> o t q", q=4), yp.rearrange("o (t q) -> o t q", q=4)).then_inc(y_ready, 1)

            for n in range(2 * NB):
                copy_block(0, n)
            gram_turn(0, True)
            z_copy(0, True)

            def group(g, first_mlp):
                for n in range(2 * NB):
                    copy_block(g, n)
                    if n == 2:
                        relu1(g - 1, first_mlp)
                    if n == 7:
                        relu2(g - 1, first_mlp)
                    if n == 11:
                        y_copy(g - 1)
                gram_turn(g, False)
                z_copy(g, False)

            group(1, True)
            with act.Fori(2, G) as g:
                group(g, False)
            relu1(G - 1, False)
            relu2(G - 1, False)
            y_copy(G - 1)


_INS = (["dense_ctx", "ids"] + [f"tbl_{f}" for f in range(NF)]
        + ["W_top1", "b_top1", "W_top2", "b_top2", "W_top3", "L0_rec_W1", "L0_rec_b1", "L0_rec_W2", "L0_rec_b2"])


def kernel(**inputs):
    import numpy as _np
    import concourse.bacc as _bacc
    from concourse import mybir as _mybir
    from concourse.bass_utils import run_bass_kernel_spmd as _run

    nc = _bacc.Bacc("TRN2", target_bir_lowering=False, num_devices=1)
    arrays, args = {}, {}
    for name in _INS:
        x = _np.ascontiguousarray(inputs[name])
        arrays[f"in_{name}"] = x
        args[name] = nc.dram_tensor(f"in_{name}", x.shape, _mybir.dt.from_np(x.dtype), kind="ExternalInput").ap()
    y = nc.dram_tensor("out_y", (B, 1), _mybir.dt.float32, kind="ExternalOutput").ap()
    build(nc, args, y)
    r = _run(nc, [arrays], core_ids=[0])
    return r.results[0]["out_y"]
```

```python
from contextlib import ExitStack

import concourse.bass as bass
from concourse import mybir
from concourse.alu_op_type import AluOpType as ALU


F32 = mybir.dt.float32
BF16 = mybir.dt.bfloat16
I32 = mybir.dt.int32
ACT = mybir.ActivationFunctionType

P = 128
NF = 26
NH = NF // 2
K = 32
B = 512
G = B // P
NT = P // 4
PARTS = ((0, NH), (NH, NF - 2), (NF - 2, NF))
Q1 = (NH + 1) // 2
Q2 = NH - Q1
NIN = NH + Q1 * (Q1 - 1) // 2 + Q2 * (Q2 - 1) // 2
SGL = NIN
ONE = SGL + NH
HALF = 64
ACR = HALF
NX = Q1 * Q2
MC = ACR + NX
assert ONE + 2 == HALF
BLK = 4
NB = NT // BLK
L3_AT = 1
WARM_CTX, WARM_W2, WARM_VA = 9, 7, 7
RING = 4
MIX = NX + NH * NH
PR = NIN + NX + NIN + 1
PR_ACROSS, PR_OWN, PR_ONE = NIN, NIN + NX, PR - 1
GR = NH * NF + NH * NH
GCH = (127, 128, 126, 126)
GC = len(GCH)
GOFF = tuple(sum(GCH[:i]) for i in range(GC))
assert sum(GCH) == GR and GOFF[2] <= NH * NF and GCH[2] == GCH[3]
H = 128
CTX = 16
SLOTS = P // CTX
CTX_SLOTS = ("hi", "mid", "lo", None, "hi", "mid", "hi", None)
D1, D2 = 512, 256
M1, M2 = D1 // P, D2 // P


def inner_pairs():
    at, out = NH, []
    for q_first, q_end in ((0, Q1), (Q1, NH)):
        for p in range(q_first, q_end - 1):
            n = q_end - 1 - p
            out.append((at, p, p + 1, n))
            at += n
    assert at == NIN
    return out


def build(nc, a, y):
    with ExitStack() as ctx:
        def sb(name, shape, dt=F32):
            return ctx.enter_context(nc.sbuf_tensor(name, shape, dt))

        def sem(name):
            return ctx.enter_context(nc.semaphore(name))

        idx = sb("idx", [P, G, NF], I32)
        emb = sb("emb", [P, G, NF * K])
        ework = sb("ework", [P, NF * K])
        L = [sb(f"l_{x}", [P, NT, MC]) for x in "ab"]
        R = sb("r", [P, NT, 4, NF])
        t_a = sb("t_a", [P, NF, P])
        t_b = sb("t_b", [P, NH, P])
        gram = sb("gram", [P, GC, P])
        ident = sb("ident", [P, P])
        w1 = sb("w1", [P, NF, NF])
        w2_room = sb("w2_room", [P, NF * PR])
        w2 = w2_room[:, 0:H * NF].rearrange("p (i j) -> p i j", j=NF)
        prod = w2_room[:, :].rearrange("p (j w) -> p j w", w=PR)
        w2t = sb("w2t", [P, NF, H])
        w1s = sb("w1s", [P, 2 * PR + MIX + NX])
        w1p = [w1s[:, 0:PR], w1s[:, PR + MIX + NX:]]
        w1x = [w1s[:, PR:PR + NX], w1s[:, PR + MIX:PR + MIX + NX]]
        w1ab = w1s[:, PR + NX:PR + MIX].rearrange("p (u v) -> p u v", v=NH)
        w1_of = [w1s[:, 0:PR + MIX], w1s[:, PR + NX:]]
        w1g = sb("w1g", [P, GR])
        mix = sb("mix", [P, NF, MIX])
        vh = [sb(f"vh_{x}", [P, NH, MC]) for x in "ab"]
        vh_own = sb("vh_own", [P, NH, P])
        v_a = sb("v_a", [P, NF, H])
        v_b = sb("v_b", [P, NH, H])
        wg = sb("wg", [P, GC, H])
        rows = sb("rows", [10, P])
        cols = sb("cols", [P, 10])
        kb = sb("kb", [P, 2])
        ctx_in = sb("ctx_in", [P, G, CTX])
        ctx_part = sb("ctx_part", [P, G, CTX], BF16)
        ctx_rest = [sb(f"ctx_rest{i}", [P, G, CTX]) for i in range(2)]
        ctx_x = sb("ctx_x", [P, G, SLOTS, CTX])
        ctx_t = sb("ctx_t", [P, G, P], BF16)
        wt1 = sb("wt1", [P, 2, D1])
        wt1c_in = sb("wt1c_in", [P, D1])
        wt1c_mid = sb("wt1c_mid", [P, D1], BF16)
        wt1c_rest = [sb(f"wt1c_rest{i}", [P, D1]) for i in range(2)]
        wt1c = sb("wt1c", [P, D1], BF16)
        wt2 = sb("wt2", [P, M1, D2])
        z = sb("z", [P, 2, P])
        h1 = sb("h1", [P, M1, P])
        h2 = sb("h2", [P, M2, P])
        yrow = sb("yrow", [1, B])
        gram_dram = nc.dram_tensor("gram_scratch", [GR, P], F32, kind="Internal").ap()

        ring = [ctx.enter_context(nc.psum_tensor(f"ring{i}", [P, 512], F32)) for i in range(RING)]
        zp = [ctx.enter_context(nc.psum_tensor(f"z{i + 1}p", [P, 512], F32))[:, 0:P] for i in range(2)]
        h1p = ctx.enter_context(nc.psum_tensor("h1p", [P, M1, P], F32))
        h2y = ctx.enter_context(nc.psum_tensor("h2y", [P, 4, P], F32))
        h2p, yp = [h2y[:, m, :] for m in range(M2)], h2y[0:1, M2, :]
        h2_tail, y_tail = [h1p[:, 0, :], h2p[1]], zp[0][0:1, :]
        h1_tail = [bank[:, 0:P] for bank in ring]

        ids_in = sem("ids_in")
        w2_in = sem("w2_in")
        w1_in = sem("w1_in")
        rows_in = sem("rows_in")
        ctx_loaded = sem("ctx_loaded")
        wt_in = sem("wt_in")
        wt1c_loaded = sem("wt1c_loaded")
        gathered = [[sem(f"gathered{g}_{c}") for c in range(3)] for g in range(G)]
        part_in = sem("part_in")
        ident_step = sem("ident_step")
        ctx_split = sem("ctx_split")
        wt1c_split = sem("wt1c_split")
        pre_done = sem("pre_done")
        pre_out = sem("pre_out")
        w1_ready = sem("w1_ready")
        vh_mixed = sem("vh_mixed")
        vh_ready = sem("vh_ready")
        zeroed = sem("zeroed")
        e_moved = sem("e_moved")
        singles = sem("singles")
        r_ready = sem("r_ready")
        pairs = sem("pairs")
        t_done = sem("t_done")
        t_out = sem("t_out")
        gram_a_stored = sem("gram_a_stored")
        gram_b_stored = sem("gram_b_stored")
        gram_in = sem("gram_in")
        z2_done = sem("z2_done")
        z1_done = sem("z1_done")
        z1_ready = sem("z1_ready")
        z2_ready = sem("z2_ready")
        h1_done = sem("h1_done")
        h1_ready = sem("h1_ready")
        h2_done = sem("h2_done")
        h2_ready = sem("h2_ready")
        y_done = sem("y_done")
        y_ready = sem("y_ready")
        y_out = sem("y_out")
        kb_ready = sem("kb_ready")

        def cut(count, most):
            return [(j, min(most, count - j)) for j in range(0, count, most)]

        pre = [("ctx", 0, 0)] + [("w2t", j, n) for j, n in cut(NF, 4)] + [("small", 0, 0)]
        pre += [("mix", x, 1) for x in range(NF)]
        pre += [("wg", 0, 0)]
        pre += [("va", j, n) for j, n in cut(NH, 4)]
        EARLY = len(pre)
        pre += [("vb", j, n) for j, n in cut(NH, 4)]
        LATE = len(pre)
        pre += [("own", j, n) for j, n in cut(NH, 4)]
        at = {b: n for n, b in enumerate(pre)}

        def pre_bank(n):
            return ring[(n if n < EARLY else n - EARLY) % RING]

        def w2t_out(j):
            return at[("w2t",) + cut(NF, 4)[j // 4]] + 1

        MIX_OUT = [at[("mix", NH - 1, 1)] + 1, at[("mix", NF - 1, 1)] + 1]

        block = ctx.enter_context(nc.Block())

        @block.sync
        def _(sp):
            sp.dma_start(idx[:, :, :], a["ids"].rearrange("(g p) f -> p g f", p=P)).then_inc(ids_in, 16)
            sp.dma_start(w2[:, :, :], a["L0_rec_W2"]).then_inc(w2_in, 16)
            sp.dma_start(w1[:, :, :], a["L0_rec_W1"]).then_inc(w1_in, 16)
            sp.dma_start(wt1[:, :, :], a["W_top1"][0:2 * P, :].rearrange("(c p) n -> p c n", p=P)).then_inc(wt_in, 16)
            for s in range(SLOTS):
                sp.dma_start(wt1c_in[s * CTX:(s + 1) * CTX, :], a["W_top1"][2 * P:2 * P + CTX, :]).then_inc(wt1c_loaded, 16)
            sp.dma_start(wt2[:, :, :], a["W_top2"].rearrange("(c p) n -> p c n", p=P)).then_inc(wt_in, 16)
            for g in range(G):
                for c, (f0, f1) in enumerate(PARTS):
                    sp.wait_ge(gathered[g][c], 16 * (f1 - f0))
                    sp.sem_inc(part_in, 1)
            sp.wait_ge(y_ready, G)
            sp.dma_start(y.rearrange("b o -> o b"), yrow[:, :]).then_inc(y_out, 16)
            sp.wait_ge(y_out, 16)

        @block.gpsimd
        def _(pool):
            pool.memset(ident[:, :], 0.0).then_inc(ident_step, 1)
            pool.wait_ge(ident_step, 1)
            pool.affine_select(out=ident[:, :], in_=ident[:, :], compare_op=ALU.not_equal, fill=1.0, base=0,
                               pattern=[[-1, P]], channel_multiplier=1).then_inc(ident_step, 1)
            pool.wait_ge(ids_in, 16)
            for g in range(G):
                for f in range(NF):
                    part = [c for c, (f0, f1) in enumerate(PARTS) if f0 <= f < f1][0]
                    pool.indirect_dma_start(
                        out=emb[:, g, f * K:(f + 1) * K], out_offset=None, in_=a[f"tbl_{f}"][:, :],
                        in_offset=bass.IndirectOffsetOnAxis(ap=idx[:, g, f:f + 1], axis=0),
                    ).then_inc(gathered[g][part], 16)

        @block.vector
        def _(dve):
            dve.memset(ctx_x[:, :, :, :], 0.0).then_inc(ctx_split, 1)
            for c in range(2):
                dve.memset(L[c][:, :, ONE:ONE + 1], 1.0)
                dve.memset(L[c][:, :, ONE + 1:ACR], 0.0)
                dve.memset(vh[c][:, :, SGL:ACR], 0.0)
            dve.memset(vh_own[:, :, 0:HALF], 0.0)
            dve.wait_ge(ctx_loaded, 16)
            x = ctx_in
            for n, part in enumerate(("hi", "mid", "lo")):
                dve.tensor_copy(ctx_part[:, :, :], x[:, :, :]).then_inc(ctx_split, 1)
                dve.wait_ge(ctx_split, 2 * n + 2)
                for s in range(SLOTS):
                    if CTX_SLOTS[s] == part:
                        last = dve.tensor_copy(ctx_x[:, :, s, :], ctx_part[:, :, :])
                if n < 2:
                    last = dve.tensor_tensor(ctx_rest[n][:, :, :], x[:, :, :], ctx_part[:, :, :], ALU.subtract)
                    x = ctx_rest[n]
                last.then_inc(ctx_split, 1)
                dve.wait_ge(ctx_split, 2 * n + 3)

            dve.memset(vh_own[:, :, HALF:P], 0.0)
            dve.memset(R[:, 0:NT // 2, :, :], 0.0)

            dve.wait_ge(w1_in, 16)
            dve.tensor_tensor(w1ab, w1[:, 0:NH, NH:NF], w1[:, NH:NF, 0:NH].rearrange("p v u -> p u v"), ALU.add)
            for c in range(2):
                o = c * NH
                last = dve.tensor_tensor(w1x[c].rearrange("p (u v) -> p u v", v=Q2), w1[:, o:o + Q1, o + Q1:o + NH],
                                         w1[:, o + Q1:o + NH, o:o + Q1].rearrange("p v u -> p u v"), ALU.add)
            last.then_inc(w1_ready, 1)
            dve.wait_ge(w1_ready, 1)
            w1flat = w1[:, :, :].rearrange("p u v -> p (u v)")
            for c in range(2):
                o = c * NH
                d0 = o * (NF + 1)
                pairs_of = w1p[1 - c]
                dve.tensor_copy(pairs_of[:, 0:NH], w1flat[:, d0:d0 + (NH - 1) * (NF + 1) + 1:NF + 1])
                for col, p, q, n in inner_pairs():
                    dve.tensor_tensor(pairs_of[:, col:col + n], w1[:, o + p, o + q:o + q + n],
                                      w1[:, o + q:o + q + n, o + p], ALU.add)
                last = dve.tensor_copy(pairs_of[:, PR_ACROSS:PR_OWN], w1x[c])
            last.then_inc(w1_ready, 1)
            dve.wait_ge(w1_ready, 2)
            for d in range(2):
                last = dve.tensor_copy(w1p[d][:, PR_OWN:PR_ONE], w1p[1 - d][:, 0:NIN])
            last.then_inc(w1_ready, 1)
            wga = w1g[:, 0:NH * NF].rearrange("p (u v) -> p u v", v=NF)
            dve.tensor_copy(wga[:, :, 0:NH], w1[:, 0:NH, 0:NH])
            dve.tensor_copy(wga[:, :, NH:NF], w1ab)
            dve.tensor_copy(w1g[:, NH * NF:GR].rearrange("p (u v) -> p u v", v=NH), w1[:, NH:NF, NH:NF]).then_inc(w1_ready, 1)

            def mixed(c, x0, x1, quarters):
                first, n = (0, NH * NH) if not quarters else (NH * NH, NX)
                if c == 0:
                    first = NX - first if not quarters else 0
                v = mix[:, c * NH + x0:c * NH + x1, first:first + n]
                return v.rearrange("p x (u v) -> p x u v", v=NH if not quarters else Q2)

            def mixed_terms(c):
                dve.wait_ge(pre_out, MIX_OUT[c])

                def m(x, xn, u, un):
                    v = mixed(c, x, x + xn, False)
                    return v[:, :, u:u + un, :] if c == 0 else v[:, :, :, u:u + un].rearrange("p x j u -> p x u j")

                def sums(dst, x, xn, u, un):
                    return dve.tensor_tensor(dst, m(x, xn, u, un), m(u, un, x, xn).rearrange("p q x j -> p x q j"), ALU.add)

                out = vh[c]
                for p in range(NH):
                    dve.tensor_copy(out[:, :, p], m(p, 1, p, 1).rearrange("p a b j -> p (a b j)"))
                for col, p, q, n in inner_pairs():
                    sums(out[:, :, col:col + n].rearrange("p j (x q) -> p x q j", x=1), p, 1, q, n)
                for p in range(Q1):
                    col = ACR + p * Q2
                    last = sums(out[:, :, col:col + Q2].rearrange("p j (x q) -> p x q j", x=1), p, 1, Q1, Q2)
                last.then_inc(vh_mixed, 1)

            def add_unmixed(c):
                dve.wait_ge(pre_out, MIX_OUT[1])
                dve.wait_ge(vh_mixed, c + 1)
                v, w = vh[c], prod[:, (1 - c) * NH:(2 - c) * NH, :]
                if c == 0:
                    dve.tensor_copy(v[:, :, ONE], w[:, :, PR_ONE])
                dve.tensor_tensor(v[:, :, 0:NIN], v[:, :, 0:NIN], w[:, :, 0:NIN], ALU.add)
                dve.tensor_tensor(v[:, :, ACR:MC], v[:, :, ACR:MC], w[:, :, PR_ACROSS:PR_OWN], ALU.add).then_inc(vh_ready, 1)

            def own_terms(c):
                r = c * HALF
                for quarter, (x0, x1) in enumerate(((0, Q1), (Q1, NH))):
                    js = slice(Q1, NH) if quarter == 0 else slice(0, Q1)

                    def m(x, xn, u, un):
                        v = mixed(c, x, x + xn, True)
                        u -= x0
                        return v[:, :, u:u + un, :] if quarter == 0 else v[:, :, :, u:u + un].rearrange("p x j u -> p x u j")

                    for p in range(x0, x1):
                        dve.tensor_copy(vh_own[:, js, r + p], m(p, 1, p, 1).rearrange("p a b j -> p (a b j)"))
                    for col, p, q, n in inner_pairs():
                        if x0 <= p < x1:
                            last = dve.tensor_tensor(
                                vh_own[:, js, r + col:r + col + n].rearrange("p j (x q) -> p x q j", x=1),
                                m(p, 1, q, n), m(q, n, p, 1).rearrange("p q x j -> p x q j"), ALU.add)
                last.then_inc(vh_mixed, 1)
                dve.wait_ge(vh_mixed, 3 + c)
                v, w = vh_own[:, :, r:r + HALF], prod[:, c * NH:(c + 1) * NH, :]
                if c == 0:
                    dve.tensor_copy(v[:, :, ONE], w[:, :, PR_ONE])
                dve.tensor_tensor(v[:, :, 0:NIN], v[:, :, 0:NIN], w[:, :, PR_OWN:PR_ONE], ALU.add).then_inc(vh_ready, 1)

            def take_part(g, part, looped):
                f0, f1 = PARTS[part]
                c = f0 // NH
                o = f0 - c * NH
                e = slice(f0 * K, f1 * K)
                first = not looped and g == 0
                dve.wait_ge(part_in, 3 * g + part + 1)
                if looped:
                    src = ework[:, e]
                    dve.wait_ge(singles, 3 * g + part - 2)
                    dve.tensor_copy(src, emb[:, bass.ds(g, 1), e].rearrange("p a n -> p (a n)")).then_inc(e_moved, 1)
                    dve.wait_ge(e_moved, 3 * (g - 1) + part + 1)
                else:
                    src = emb[:, g, e]
                if not first and part < 2:
                    dve.wait_ge(t_done, 2 * NB * (g - 1) + NB * (c + 1))
                sg = L[c][:, :, SGL + o:SGL + o + f1 - f0]
                dve.transpose(sg.rearrange("p t f -> p f t"), src).then_inc(singles, 1)
                if not first and part == 0:
                    dve.wait_ge(t_done, 2 * NB * g)
                dve.wait_ge(singles, 3 * g + part + 1)
                for q in range(4):
                    s = slice(K * q, K * (q + 1))
                    last = dve.tensor_copy(R[s, :, q, f0:f1], L[c][s, :, SGL + o:SGL + o + f1 - f0])
                last.then_inc(r_ready, 1)

            def squares(c, f0, f1):
                sg = L[c][:, :, SGL + f0:SGL + f1]
                return dve.tensor_tensor(L[c][:, :, f0:f1], sg, sg, ALU.mult)

            def products(c, runs):
                for col, p, q, n in runs:
                    last = dve.tensor_tensor(L[c][:, :, col:col + n], L[c][:, :, SGL + q:SGL + q + n],
                                             L[c][:, :, SGL + p:SGL + p + 1].to_broadcast([P, NT, n]), ALU.mult)
                return last

            inner = inner_pairs()
            across = [(ACR + p * Q2, p, Q1, Q2) for p in range(Q1)]

            def build_a(g, looped):
                take_part(g, 0, looped)
                squares(0, 0, NH)
                products(0, inner + across).then_inc(pairs, 1)

            def build_b(g, looped):
                take_part(g, 1, looped)
                take_part(g, 2, looped)
                squares(1, 0, NH)
                products(1, inner + across).then_inc(pairs, 1)

            def split_wt1c():
                mid, lo = slice(P // 2, 3 * P // 4), slice(3 * P // 4, P)
                low = slice(P // 2, P)
                dve.wait_ge(wt1c_loaded, 16 * SLOTS)
                dve.tensor_copy(wt1c[:, :], wt1c_in[:, :]).then_inc(wt1c_split, 1)
                dve.wait_ge(wt1c_split, 1)
                dve.tensor_tensor(wt1c_rest[0][low, :], wt1c_in[low, :], wt1c[low, :], ALU.subtract).then_inc(wt1c_split, 1)
                dve.wait_ge(wt1c_split, 2)
                dve.tensor_copy(wt1c[mid, :], wt1c_rest[0][mid, :])
                dve.tensor_copy(wt1c_mid[lo, :], wt1c_rest[0][lo, :]).then_inc(wt1c_split, 1)
                dve.wait_ge(wt1c_split, 3)
                dve.tensor_tensor(wt1c_rest[1][lo, :], wt1c_rest[0][lo, :], wt1c_mid[lo, :], ALU.subtract).then_inc(wt1c_split, 1)
                dve.wait_ge(wt1c_split, 4)
                dve.tensor_copy(wt1c[lo, :], wt1c_rest[1][lo, :]).then_inc(wt1c_split, 1)

            dve.memset(R[:, NT // 2:NT, :, :], 0.0).then_inc(zeroed, 1)
            split_wt1c()
            dve.wait_ge(zeroed, 1)
            build_a(0, False)
            mixed_terms(0)
            add_unmixed(0)
            build_b(0, False)
            mixed_terms(1)
            add_unmixed(1)
            own_terms(0)
            own_terms(1)
            with dve.Fori(1, G - 1) as g:
                build_a(g, True)
                build_b(g, True)
            build_a(G - 1, False)
            build_b(G - 1, False)

        @block.tensor
        def _(pe):
            def keep_warm(count):
                for _ in range(count):
                    pe.matmul(zp[0], ident[:, :], ident[:, :], start=True, stop=True)

            def prepare(n):
                kind, c, m = pre[n]
                ps = pre_bank(n)
                if n >= EARLY + RING or RING <= n < EARLY:
                    pe.wait_ge(pre_out, n - RING + 1)
                elif n >= EARLY:
                    pe.wait_ge(t_out, 2 * NB - RING + n - EARLY + 1)
                if kind == "small":
                    pe.wait_ge(rows_in, 16 * 5)
                    last = pe.transpose(ps[:, 0:10], rows[:, :], ident[0:10, 0:10])
                elif kind == "w2t":
                    if c == 0:
                        keep_warm(WARM_W2)
                        pe.wait_ge(w2_in, 16)
                    for i in range(m):
                        last = pe.transpose(ps[:, i * H:(i + 1) * H], w2[:, :, c + i], ident[:, :])
                elif kind == "ctx":
                    keep_warm(WARM_CTX)
                    pe.wait_ge(ctx_split, 7)
                    for g in range(G):
                        last = pe.transpose(ps[:, g * P:(g + 1) * P], ctx_x[:, g, :, :].rearrange("p s c -> p (s c)"), ident[:, :])
                elif kind == "mix":
                    if c == 0:
                        pe.wait_ge(w1_ready, 3)
                        pe.wait_ge(pre_out, at[("small", 0, 0)] + 1)
                    pe.wait_ge(pre_out, w2t_out(c))
                    last = pe.matmul(ps[:, 0:PR + MIX], w2t[:, c, :], w1_of[c // NH], start=True, stop=True)
                elif kind == "wg":
                    pe.wait_ge(w1_ready, 4)
                    for i in range(GC):
                        w = GCH[i]
                        last = pe.transpose(ps[0:w, i * H:(i + 1) * H], w1g[:, GOFF[i]:GOFF[i] + w], ident[:, :])
                else:
                    if c == 0:
                        if kind == "va":
                            keep_warm(WARM_VA)
                        pe.wait_ge(vh_ready, {"va": 1, "vb": 2, "own": 4}[kind])
                    v = {"va": vh[0], "vb": vh[1], "own": vh_own}[kind]
                    for i in range(m):
                        last = pe.transpose(ps[0:v.shape[2], i * H:(i + 1) * H], v[:, c + i, :], ident[:, :])
                last.then_inc(pre_done, 1)

            def t_block(g, n, first):
                c, blk = divmod(n, NB)
                if blk == 0:
                    pe.wait_ge(pairs, 2 * g + c + 1)
                    if c == 0:
                        pe.wait_ge(r_ready, 3 * (g + 1))
                if first and n < RING:
                    pe.wait_ge(pre_out, EARLY - (EARLY - 1 - n) % RING)
                else:
                    pe.wait_ge(t_out, 2 * NB * g + n - RING + 1)
                ps = ring[n % RING]
                for i in range(BLK):
                    t = blk * BLK + i
                    last = pe.matmul(ps[0:MC, i * 4 * NF:(i + 1) * 4 * NF], L[c][:, t, :],
                                     R[:, t, :, :].rearrange("p q f -> p (q f)"), start=True, stop=True)
                last.then_inc(t_done, 1)

            def gram_part(g):
                pe.wait_ge(gram_in, 48 * (g + 1))
                for i in range(GC):
                    w = GCH[i]
                    last = pe.matmul(zp[0], wg[0:w, i, :], gram[0:w, i, :], start=(i == 0), stop=(i == GC - 1))
                last.then_inc(z1_done, 1)

            def z_group(g, first, tail=False):
                pe.wait_ge(t_out, 2 * NB * g + NB)
                for j in range(NH, NF):
                    pe.matmul(zp[1], v_a[0:MC, j, :], t_a[0:MC, j, :], start=(j == NH), stop=False)
                pe.wait_ge(t_out, 2 * NB * (g + 1))
                if first:
                    pe.wait_ge(pre_out, LATE)
                for j in range(NH):
                    pe.matmul(zp[1], v_b[0:MC, j, :], t_b[0:MC, j, :], start=False, stop=False)

                def own():
                    for j in range(NH):
                        last = pe.matmul(zp[1], v_a[:, j, :], t_a[:, j, :], start=False, stop=(j == NH - 1))
                    last.then_inc(z2_done, 1)

                if first:
                    for n in range(LATE, len(pre)):
                        prepare(n)
                    gram_part(g)
                    pe.wait_ge(pre_out, len(pre))
                    own()
                    return
                if not tail:
                    own()
                    gram_part(g)
                    return
                gram_part(g)
                own()
                pe.wait_ge(z1_ready, g + 1)
                for m in range(M1):
                    pe.matmul(h1_tail[m], wt1c[:, m * P:(m + 1) * P], ctx_t[:, g, :], start=True, stop=False)
                    pe.matmul(h1_tail[m], wt1[:, 0, m * P:(m + 1) * P], z[:, 0, :], start=False, stop=False)
                pe.wait_ge(z2_ready, g + 1)
                for m in range(M1):
                    pe.matmul(h1_tail[m], wt1[:, 1, m * P:(m + 1) * P], z[:, 1, :],
                              start=False, stop=True).then_inc(h1_done, 1)

            def layer1(g):
                pe.wait_ge(z1_ready, g + 1)
                pe.wait_ge(z2_ready, g + 1)
                for m in range(M1):
                    s = slice(m * P, (m + 1) * P)
                    cg = ctx_t[:, g, :] if isinstance(g, int) else ctx_t[:, bass.ds(g, 1), :].rearrange("p a n -> p (a n)")
                    pe.matmul(h1p[:, m, :], wt1c[:, s], cg, start=True, stop=False)
                    pe.matmul(h1p[:, m, :], wt1[:, 0, s], z[:, 0, :], start=False, stop=False)
                    last = pe.matmul(h1p[:, m, :], wt1[:, 1, s], z[:, 1, :], start=False, stop=True)
                last.then_inc(h1_done, 1)

            def layer2(g, out, tail=False):
                for m in range(M2):
                    for kc in range(M1):
                        if m == 0:
                            pe.wait_ge(h1_ready, M1 * g + kc + 1)
                        last = pe.matmul(out[m], wt2[:, kc, m * P:(m + 1) * P], h1[:, kc, :],
                                         start=(kc == 0), stop=(kc == M1 - 1))
                    if tail or m == M2 - 1:
                        last.then_inc(h2_done, 1)

            def layer3(g, out, tail=False):
                if not tail:
                    pe.wait_ge(h2_ready, M2 * (g + 1))
                for kc in range(M2):
                    if tail:
                        pe.wait_ge(h2_ready, M2 * g + kc + 1)
                    last = pe.matmul(out, cols[:, 6 + kc:7 + kc], h2[:, kc, :], start=(kc == 0), stop=(kc == M2 - 1))
                last.then_inc(y_done, 1)

            pe.wait_ge(ident_step, 2)
            for n in range(EARLY):
                prepare(n)
            for n in range(2 * NB):
                t_block(0, n, True)
            for n in range(EARLY, LATE):
                prepare(n)
            z_group(0, True)
            pe.wait_ge(wt_in, 32)
            pe.wait_ge(wt1c_split, 5)
            with pe.Fori(1, G - 1) as g:
                layer1(g - 1)
                layer2(g - 1, h2p)
                for n in range(2 * NB):
                    t_block(g, n, False)
                    if n == L3_AT:
                        layer3(g - 1, yp)
                z_group(g, False)
            layer1(G - 2)
            layer2(G - 2, h2p)
            for n in range(2 * NB):
                t_block(G - 1, n, False)
                if n == L3_AT:
                    layer3(G - 2, yp)
            z_group(G - 1, False, tail=True)
            pe.wait_ge(y_ready, G - 1)
            layer2(G - 1, h2_tail, tail=True)
            layer3(G - 1, y_tail, tail=True)

        @block.scalar
        def _(act):
            act.dma_start(ctx_in[:, :, :], a["dense_ctx"].rearrange("(g p) c -> p g c", p=P)).then_inc(ctx_loaded, 16)
            act.dma_start(rows[0:4, :], a["b_top1"].rearrange("(r n) -> r n", n=P)).then_inc(rows_in, 16)
            act.dma_start(rows[4:6, :], a["b_top2"].rearrange("(r n) -> r n", n=P)).then_inc(rows_in, 16)
            act.dma_start(rows[6:8, :], a["W_top3"].rearrange("(r n) o -> r (n o)", n=P)).then_inc(rows_in, 16)
            act.dma_start(rows[8:9, :], a["L0_rec_b1"].rearrange("(r n) -> r n", n=P)).then_inc(rows_in, 16)
            act.dma_start(rows[9:10, :], a["L0_rec_b2"].rearrange("(r n) -> r n", n=P)).then_inc(rows_in, 16)

            def take_out(n):
                kind, c, m = pre[n]
                ps = pre_bank(n)
                act.wait_ge(pre_done, n + 1)
                if kind == "small":
                    for d in range(2):
                        act.copy(w1p[d][:, PR_ONE:PR], ps[:, 8:9])
                    last = act.copy(cols[:, :], ps[:, 0:10])
                elif kind == "w2t":
                    last = act.copy(w2t[:, c:c + m, :].rearrange("p j h -> p (j h)"), ps[:, 0:m * H])
                elif kind == "ctx":
                    for g in range(G):
                        last = act.copy(ctx_t[:, g, :].rearrange("p (t q) -> p t q", q=4),
                                        ps[:, g * P:(g + 1) * P].rearrange("p (q t) -> p t q", q=4))
                elif kind == "mix":
                    unmixed, mixed = (0, PR) if c < NH else (MIX, 0)
                    act.copy(prod[:, c, :], ps[:, unmixed:unmixed + PR])
                    last = act.copy(mix[:, c, :], ps[:, mixed:mixed + MIX])
                elif kind == "wg":
                    for i in range(GC):
                        last = act.copy(wg[0:GCH[i], i, :], ps[0:GCH[i], i * H:(i + 1) * H])
                else:
                    r = P if kind == "own" else MC
                    dst = {"va": v_a[0:r, NH + c:NH + c + m, :], "vb": v_b[0:r, c:c + m, :], "own": v_a[:, c:c + m, :]}[kind]
                    last = act.copy(dst.rearrange("p j h -> p (j h)"), ps[0:r, 0:m * H])
                last.then_inc(pre_out, 1)

            for n in range(EARLY):
                take_out(n)
            act.mul(kb[:, :], cols[:, 8:10], float(K)).then_inc(kb_ready, 1)
            act.wait_ge(kb_ready, 1)

            def copy_block(g, n):
                c, blk = divmod(n, NB)
                act.wait_ge(t_done, 2 * NB * g + n + 1)
                src = ring[n % RING][:, 0:BLK * 4 * NF].rearrange("p (x j) -> p j x", j=NF)
                s = slice(blk * 4 * BLK, (blk + 1) * 4 * BLK)
                if c == 0:
                    act.copy(t_a[0:MC, :, s], src[0:MC, :, :]).then_inc(t_out, 1)
                else:
                    act.copy(t_b[0:MC, :, s], src[0:MC, 0:NH, :])
                    act.wait_ge(t_out, 2 * NB * g + blk + 1)
                    act.copy(t_a[HALF:P, 0:NH, s], src[0:HALF, NH:NF, :]).then_inc(t_out, 1)

            def gram_a_out(g):
                act.wait_ge(t_out, 2 * NB * g + NB)
                act.dma_start(gram_dram[0:NH * NF, :].rearrange("(u v) b -> u v b", v=NF),
                              t_a[SGL:SGL + NH, :, :]).then_inc(gram_a_stored, 16)

            def gram_turn(g):
                act.wait_ge(t_out, 2 * NB * (g + 1))
                act.dma_start(gram_dram[NH * NF:GR, :].rearrange("(u v) b -> u v b", v=NH),
                              t_a[HALF + SGL:HALF + SGL + NH, 0:NH, :]).then_inc(gram_b_stored, 16)
                act.wait_ge(gram_a_stored, 16 * (g + 1))
                for i in range(2):
                    act.dma_start(gram[0:GCH[i], i, :], gram_dram[GOFF[i]:GOFF[i] + GCH[i], :]).then_inc(gram_in, 16)
                act.wait_ge(gram_b_stored, 16 * (g + 1))
                act.dma_start(gram[0:GCH[2], 2:GC, :],
                              gram_dram[GOFF[2]:GR, :].rearrange("(c p) b -> p c b", c=2)).then_inc(gram_in, 16)

            def z_copy(g, order):
                done, ready = (z1_done, z2_done), (z1_ready, z2_ready)
                for i in order:
                    act.wait_ge(done[i], g + 1)
                    act.activation(z[:, i, :], zp[i], ACT.Identity, bias=kb[:, i:i + 1]).then_inc(ready[i], 1)

            def relu1(g):
                act.wait_ge(h1_done, g + 1)
                for m in range(M1):
                    act.activation(h1[:, m, :], h1p[:, m, :], ACT.Relu, bias=cols[:, m:m + 1]).then_inc(h1_ready, 1)

            def relu2(g):
                act.wait_ge(h2_done, g + 1)
                for m in range(M2):
                    act.activation(h2[:, m, :], h2p[m], ACT.Relu, bias=cols[:, 4 + m:5 + m]).then_inc(h2_ready, 1)

            def y_copy(g, src):
                act.wait_ge(y_done, g + 1)
                yg = yrow[:, g * P:(g + 1) * P] if isinstance(g, int) else yrow[:, bass.ds(g * P, P)]
                act.copy(yg.rearrange("o (q t) -> o t q", q=4), src.rearrange("o (t q) -> o t q", q=4)).then_inc(y_ready, 1)

            for n in range(2 * NB):
                copy_block(0, n)
                if n == NB:
                    gram_a_out(0)
            for n in range(EARLY, LATE):
                take_out(n)
            gram_turn(0)
            for n in range(LATE, len(pre)):
                take_out(n)
            z_copy(0, (0, 1))

            def group(g):
                relu1(g - 1)
                relu2(g - 1)
                for n in range(2 * NB):
                    copy_block(g, n)
                    if n == NB:
                        gram_a_out(g)
                    if n == L3_AT:
                        y_copy(g - 1, yp)
                gram_turn(g)

            with act.Fori(1, G - 1) as g:
                group(g)
                z_copy(g, (1, 0))
            group(G - 1)
            z_copy(G - 1, (0, 1))
            for m in range(M1):
                act.wait_ge(h1_done, G - 1 + m + 1)
                act.activation(h1[:, m, :], h1_tail[m], ACT.Relu, bias=cols[:, m:m + 1]).then_inc(h1_ready, 1)
            for m in range(M2):
                act.wait_ge(h2_done, G - 1 + m + 1)
                act.activation(h2[:, m, :], h2_tail[m], ACT.Relu, bias=cols[:, 4 + m:5 + m]).then_inc(h2_ready, 1)
            y_copy(G - 1, y_tail)


_INS = (["dense_ctx", "ids"] + [f"tbl_{f}" for f in range(NF)]
        + ["W_top1", "b_top1", "W_top2", "b_top2", "W_top3", "L0_rec_W1", "L0_rec_b1", "L0_rec_W2", "L0_rec_b2"])


def kernel(**inputs):
    import numpy as _np
    import concourse.bacc as _bacc
    from concourse import mybir as _mybir
    from concourse.bass_utils import run_bass_kernel_spmd as _run

    nc = _bacc.Bacc("TRN2", target_bir_lowering=False, num_devices=1)
    arrays, args = {}, {}
    for name in _INS:
        x = _np.ascontiguousarray(inputs[name])
        arrays[f"in_{name}"] = x
        args[name] = nc.dram_tensor(f"in_{name}", x.shape, _mybir.dt.from_np(x.dtype), kind="ExternalInput").ap()
    y = nc.dram_tensor("out_y", (B, 1), _mybir.dt.float32, kind="ExternalOutput").ap()
    build(nc, args, y)
    r = _run(nc, [arrays], core_ids=[0])
    return r.results[0]["out_y"]
```
